# Optimizing a Trainium2 kernel written in Bass

```python
import numpy as np
import jax
import jax.numpy as jnp

def _softmax(x, axis=-1):
    return jax.nn.softmax(x, axis=axis)

def _gelu(x):
    return jax.nn.gelu(x, approximate=True)

def _silu(x):
    return jax.nn.silu(x)

def _sigmoid(x):
    return jax.nn.sigmoid(x)

def _layernorm(x, axis=-1, eps=1e-05):
    m = jnp.mean(x, axis=axis, keepdims=True)
    v = jnp.var(x, axis=axis, keepdims=True)
    return (x - m) / jnp.sqrt(v + eps)

def _scatter_add(tgt, idx, src, axis=0):
    return tgt.at[idx].add(src)

def _segment_sum(src, seg, n):
    return jax.ops.segment_sum(src, seg, n)
kernel_name = 'mk_xattn_seq_d4_seqx_r4_372f8c'

def setup_inputs(seed: int=0):
    np.random.seed(seed)
    _w = jnp.asarray

    def _rec_inputs():
        import jax
        import jax.numpy as jnp
        _rk = jax.random.key(seed)
        x = 7.22e-05 + 1 * jax.random.normal(jax.random.fold_in(_rk, 1), (16, 256, 256), jnp.float32)
        _lenS = 256 - jax.random.randint(jax.random.fold_in(_rk, 7), (16,), 0, max(1, 256 // 4) + 1, jnp.int32)
        _lenS2 = 256 - jax.random.randint(jax.random.fold_in(_rk, 8), (16,), 0, max(1, 256 // 4) + 1, jnp.int32)
        _ctx_1024P = jax.random.normal(jax.random.fold_in(_rk, 11), (16, 16, 256), jnp.float32)
        _ctx_1024c = jax.random.dirichlet(jax.random.fold_in(_rk, 511), 0.3 * jnp.ones((16,), jnp.float32), (16, 256))
        _ctx_1024t = jnp.einsum('bsk,bkd->bsd', _ctx_1024c, _ctx_1024P)
        _ctx_1024t = _ctx_1024t * jax.lax.rsqrt(jnp.mean(jnp.square(_ctx_1024t)) + 1e-12) * 0.953939
        ctx_1024 = 4.13588e-05 + 0.999923 * (_ctx_1024t + 0.3 * jax.random.normal(jax.random.fold_in(_rk, 611), (16, 256, 256), jnp.float32))
        _validS = jnp.arange(256)[None, :] < _lenS[:, None]
        _validS2 = jnp.arange(256)[None, :] < _lenS2[:, None]
        _causal = jnp.tril(jnp.ones((256, 256), dtype=bool))
        mask_1x1xSxS2_ik0 = jnp.where(jnp.broadcast_to(_validS2[0:1, None, None, :], (1, 1, 256, 256)), 0, 1).astype(jnp.int32)
        mask_Bx1x1xS2_ik0 = jnp.where(jnp.broadcast_to(_validS2[:, None, None, :], (16, 1, 1, 256)), 0, 1).astype(jnp.int32)
        return (x, ctx_1024, mask_1x1xSxS2_ik0, mask_Bx1x1xS2_ik0)
    x, ctx_1024, mask_1x1xSxS2_ik0, mask_Bx1x1xS2_ik0 = _rec_inputs()

    def _L0_xattn_setup():
        import jax, jax.numpy as jnp
        import numpy as np
        from math import sqrt
        B, S, D, H = (4, 512, 256, 16)
        HD = D // H

        def _mha(q, k, v, Wq, bq, Wk, bk, Wv, bv, Wo, bo, gamma, beta, attn_mask, pad_mask):
            seq = q.shape[1]
            x = jax.lax.stop_gradient(q)
            qp = (q @ Wq.T + bq).reshape(-1, H, seq, HD)
            kp = (k @ Wk.T + bk).reshape(-1, H, seq, HD)
            vp = (v @ Wv.T + bv).reshape(-1, H, seq, HD)
            scores = jnp.einsum('bhqd,bhkd->bhqk', qp, kp)
            scores = jnp.where(pad_mask == 0, -jnp.inf, scores)
            scores = jnp.where(attn_mask == 0, -jnp.inf, scores)
            attn = jax.nn.softmax(scores / sqrt(HD), axis=-1)
            out = jnp.einsum('bhqk,bhkd->bhqd', attn, vp).reshape(-1, seq, D)
            out = out @ Wo.T + bo
            y = x + out
            mean = jnp.mean(y, axis=-1, keepdims=True)
            std = jnp.sqrt(jnp.mean((y - mean) ** 2, axis=-1, keepdims=True))
            return gamma * ((y - mean) / (std + 1e-08)) + beta
        key = jax.random.key(seed)
        ks = jax.random.split(key, 16)
        w = 0.02
        q = jax.random.normal(ks[0], (B, S, D), jnp.float32)
        k = jax.random.normal(ks[1], (B, S, D), jnp.float32)
        v = jax.random.normal(ks[2], (B, S, D), jnp.float32)
        attn_mask = jnp.tril(jnp.ones((S, S), jnp.int32))[None, None]
        pad_mask = jax.random.randint(ks[3], (B, 1, 1, S), 0, 2, jnp.int32)
        pad_mask = pad_mask.at[..., 0].set(1)
        params = {'Wq': jax.random.normal(ks[4], (D, D), jnp.float32) * w, 'bq': jnp.zeros((D,), jnp.float32), 'Wk': jax.random.normal(ks[5], (D, D), jnp.float32) * w, 'bk': jnp.zeros((D,), jnp.float32), 'Wv': jax.random.normal(ks[6], (D, D), jnp.float32) * w, 'bv': jnp.zeros((D,), jnp.float32), 'Wo': jax.random.normal(ks[7], (D, D), jnp.float32) * w, 'bo': jnp.zeros((D,), jnp.float32), 'gamma': jnp.ones((D,), jnp.float32), 'beta': jnp.zeros((D,), jnp.float32)}
        return dict(q=q, k=k, v=v, attn_mask=attn_mask, pad_mask=pad_mask, **params)
    _L0_xattn_all = _L0_xattn_setup()
    _L0_xattn_in = {k: v for k, v in _L0_xattn_all.items() if k in ('Wq', 'bq', 'Wk', 'bk', 'Wv', 'bv', 'Wo', 'bo', 'gamma', 'beta')}
    del _L0_xattn_all

    def _L1_xattn_setup():
        import jax, jax.numpy as jnp
        import numpy as np
        EPS = 1e-05

        def _layernorm(x, w, b):
            m = jnp.mean(x, axis=-1, keepdims=True)
            v = jnp.mean(jnp.square(x - m), axis=-1, keepdims=True)
            return (x - m) * jax.lax.rsqrt(v + EPS) * w + b
        key = jax.random.key(seed)
        ks = jax.random.split(key, 12)
        B, S, E, H = (4, 512, 256, 16)
        s = 0.02
        return {'Q': jax.random.normal(ks[0], (B, S, E), jnp.float32), 'K': jax.random.normal(ks[1], (B, S, E), jnp.float32), 'V': jax.random.normal(ks[2], (B, S, E), jnp.float32), 'in_proj_w': jax.random.normal(ks[3], (3 * E, E), jnp.float32) * s, 'in_proj_b': jax.random.normal(ks[4], (3 * E,), jnp.float32) * s, 'out_proj_w': jax.random.normal(ks[5], (E, E), jnp.float32) * s, 'out_proj_b': jax.random.normal(ks[6], (E,), jnp.float32) * s, 'w1': jax.random.normal(ks[7], (4 * E, E), jnp.float32) * s, 'b1': jax.random.normal(ks[8], (4 * E,), jnp.float32) * s, 'w2': jax.random.normal(ks[9], (E, 4 * E), jnp.float32) * s, 'b2': jax.random.normal(ks[10], (E,), jnp.float32) * s, 'ln1_w': jnp.ones((E,), jnp.float32), 'ln1_b': jnp.zeros((E,), jnp.float32), 'ln2_w': jnp.ones((E,), jnp.float32), 'ln2_b': jnp.zeros((E,), jnp.float32), 'num_heads': H}
    _L1_xattn_all = _L1_xattn_setup()
    _L1_xattn_in = {k: v for k, v in _L1_xattn_all.items() if k in ('in_proj_w', 'in_proj_b', 'out_proj_w', 'out_proj_b', 'w1', 'b1', 'w2', 'b2', 'ln1_w', 'ln1_b', 'ln2_w', 'ln2_b')}
    del _L1_xattn_all

    def _L2_xattn_setup():
        import jax, jax.numpy as jnp
        import numpy as np
        EPS = 1e-05

        def _layernorm(x, g, b):
            m = jnp.mean(x, axis=-1, keepdims=True)
            v = jnp.mean((x - m) ** 2, axis=-1, keepdims=True)
            return (x - m) / jnp.sqrt(v + EPS) * g + b

        def _mha(x, kv, Wq, Wk, Wv, mask, causal):
            m = mask[:, None]
            Q = jnp.einsum('bsd,hdk->bhsk', x, Wq) * m
            K = jnp.einsum('bsd,hdk->bhsk', kv, Wk) * m
            V = jnp.einsum('bsd,hdk->bhsk', kv, Wv) * m
            energy = jnp.einsum('bhsk,bhtk->bhst', Q, K)
            S = energy.shape[-1]
            lengths = jnp.sum(energy[:, :, 0, :] != 0, axis=-1)
            cols = jnp.arange(S)
            energy = jnp.where(cols[None, None, None, :] >= lengths[:, :, None, None], -jnp.inf, energy)
            if causal:
                energy = jnp.where(cols[None, :] > cols[:, None], -jnp.inf, energy)
            dk = Wq.shape[-1]
            score = jax.nn.softmax(energy / jnp.sqrt(jnp.asarray(dk, energy.dtype)), axis=-1)
            out = jnp.einsum('bhst,bhtk->bhsk', score, V) * m
            B, H, Sx, dkk = out.shape
            return out.transpose(0, 2, 1, 3).reshape(B, Sx, H * dkk)
        key = jax.random.key(seed)
        ks = jax.random.split(key, 20)
        B, S, D, H = (2, 512, 256, 16)
        dk = D // H
        sd = 0.02
        inp = {'x': jax.random.normal(ks[0], (B, S, D), jnp.float32), 'context': jax.random.normal(ks[1], (B, S, D), jnp.float32), 'Wq1': jax.random.normal(ks[2], (H, D, dk), jnp.float32) * sd, 'Wk1': jax.random.normal(ks[3], (H, D, dk), jnp.float32) * sd, 'Wv1': jax.random.normal(ks[4], (H, D, dk), jnp.float32) * sd, 'Wq2': jax.random.normal(ks[5], (H, D, dk), jnp.float32) * sd, 'Wk2': jax.random.normal(ks[6], (H, D, dk), jnp.float32) * sd, 'Wv2': jax.random.normal(ks[7], (H, D, dk), jnp.float32) * sd, 'ln1_g': jnp.ones((D,), jnp.float32), 'ln1_b': jnp.zeros((D,), jnp.float32), 'ln2_g': jnp.ones((D,), jnp.float32), 'ln2_b': jnp.zeros((D,), jnp.float32), 'ln3_g': jnp.ones((D,), jnp.float32), 'ln3_b': jnp.zeros((D,), jnp.float32), 'fc1_w': jax.random.normal(ks[8], (D, D), jnp.float32) * sd, 'fc1_b': jnp.zeros((D,), jnp.float32), 'fc2_w': jax.random.normal(ks[9], (D, D), jnp.float32) * sd, 'fc2_b': jnp.zeros((D,), jnp.float32)}
        return inp
    _L2_xattn_all = _L2_xattn_setup()
    _L2_xattn_in = {k: v for k, v in _L2_xattn_all.items() if k in ('Wq1', 'Wk1', 'Wv1', 'Wq2', 'Wk2', 'Wv2', 'ln1_g', 'ln1_b', 'ln2_g', 'ln2_b', 'ln3_g', 'ln3_b', 'fc1_w', 'fc1_b', 'fc2_w', 'fc2_b')}
    del _L2_xattn_all

    def _L3_xattn_setup():
        import jax, jax.numpy as jnp
        import numpy as np
        D = 256
        H = 16
        DF = 4 * D
        LQ, LKV, B = (512, 1024, 2)
        EPS = 1e-05

        def _ln(x, g, b):
            mu = jnp.mean(x, axis=-1, keepdims=True)
            var = jnp.mean(jnp.square(x - mu), axis=-1, keepdims=True)
            return (x - mu) * jax.lax.rsqrt(var + EPS) * g + b

        def _mha(q, k, v, wq, wk, wv, wo):
            q = q @ wq.T
            k = k @ wk.T
            v = v @ wv.T
            b, lq, _ = q.shape
            lv = v.shape[1]
            qh = q.reshape(b, lq, H, -1).transpose(0, 2, 1, 3)
            kh = k.reshape(b, lv, H, -1).transpose(0, 2, 1, 3)
            vh = v.reshape(b, lv, H, -1).transpose(0, 2, 1, 3)
            dh = qh.shape[-1]
            scores = jnp.einsum('bhqd,bhkd->bhqk', qh, kh) / jnp.sqrt(jnp.float32(dh))
            attn = jax.nn.softmax(scores, axis=-1)
            o = jnp.einsum('bhqk,bhkd->bhqd', attn, vh)
            o = o.transpose(0, 2, 1, 3).reshape(b, lq, -1)
            return o @ wo.T
        key = jax.random.key(seed)
        kid = [0]

        def nrm(shape, s=1.0):
            kid[0] += 1
            return jax.random.normal(jax.random.fold_in(key, kid[0]), shape, dtype=jnp.float32) * s
        inp = {'q': nrm((B, LQ, D)), 'k': nrm((B, LKV, D)), 'v': nrm((B, LKV, D)), 'sa_wq': nrm((D, D), 0.02), 'sa_wk': nrm((D, D), 0.02), 'sa_wv': nrm((D, D), 0.02), 'sa_wo': nrm((D, D), 0.02), 'ca_wq': nrm((D, D), 0.02), 'ca_wk': nrm((D, D), 0.02), 'ca_wv': nrm((D, D), 0.02), 'ca_wo': nrm((D, D), 0.02), 'g_sa': jnp.ones((D,), jnp.float32), 'b_sa': jnp.zeros((D,), jnp.float32), 'g_qca': jnp.ones((D,), jnp.float32), 'b_qca': jnp.zeros((D,), jnp.float32), 'g_kca': jnp.ones((D,), jnp.float32), 'b_kca': jnp.zeros((D,), jnp.float32), 'g_vca': jnp.ones((D,), jnp.float32), 'b_vca': jnp.zeros((D,), jnp.float32), 'g_out': jnp.ones((D,), jnp.float32), 'b_out': jnp.zeros((D,), jnp.float32), 'ffn_w1': nrm((DF, D), 0.02), 'ffn_b1': jnp.zeros((DF,), jnp.float32), 'ffn_w2': nrm((D, DF), 0.02), 'ffn_b2': jnp.zeros((D,), jnp.float32)}
        return inp
    _L3_xattn_all = _L3_xattn_setup()
    _L3_xattn_in = {k: v for k, v in _L3_xattn_all.items() if k in ('sa_wq', 'sa_wk', 'sa_wv', 'sa_wo', 'ca_wq', 'ca_wk', 'ca_wv', 'ca_wo', 'g_sa', 'b_sa', 'g_qca', 'b_qca', 'g_kca', 'b_kca', 'g_vca', 'b_vca', 'g_out', 'b_out', 'ffn_w1', 'ffn_b1', 'ffn_w2', 'ffn_b2')}
    del _L3_xattn_all
    return {'x': x, 'ctx_1024': ctx_1024, 'mask_1x1xSxS2_ik0': mask_1x1xSxS2_ik0, 'mask_Bx1x1xS2_ik0': mask_Bx1x1xS2_ik0, 'L0_xattn_Wq': _L0_xattn_in['Wq'], 'L0_xattn_bq': _L0_xattn_in['bq'], 'L0_xattn_Wk': _L0_xattn_in['Wk'], 'L0_xattn_bk': _L0_xattn_in['bk'], 'L0_xattn_Wv': _L0_xattn_in['Wv'], 'L0_xattn_bv': _L0_xattn_in['bv'], 'L0_xattn_Wo': _L0_xattn_in['Wo'], 'L0_xattn_bo': _L0_xattn_in['bo'], 'L0_xattn_gamma': _L0_xattn_in['gamma'], 'L0_xattn_beta': _L0_xattn_in['beta'], 'L1_xattn_in_proj_w': _L1_xattn_in['in_proj_w'], 'L1_xattn_in_proj_b': _L1_xattn_in['in_proj_b'], 'L1_xattn_out_proj_w': _L1_xattn_in['out_proj_w'], 'L1_xattn_out_proj_b': _L1_xattn_in['out_proj_b'], 'L1_xattn_w1': _L1_xattn_in['w1'], 'L1_xattn_b1': _L1_xattn_in['b1'], 'L1_xattn_w2': _L1_xattn_in['w2'], 'L1_xattn_b2': _L1_xattn_in['b2'], 'L1_xattn_ln1_w': _L1_xattn_in['ln1_w'], 'L1_xattn_ln1_b': _L1_xattn_in['ln1_b'], 'L1_xattn_ln2_w': _L1_xattn_in['ln2_w'], 'L1_xattn_ln2_b': _L1_xattn_in['ln2_b'], 'L2_xattn_Wq1': _L2_xattn_in['Wq1'], 'L2_xattn_Wk1': _L2_xattn_in['Wk1'], 'L2_xattn_Wv1': _L2_xattn_in['Wv1'], 'L2_xattn_Wq2': _L2_xattn_in['Wq2'], 'L2_xattn_Wk2': _L2_xattn_in['Wk2'], 'L2_xattn_Wv2': _L2_xattn_in['Wv2'], 'L2_xattn_ln1_g': _L2_xattn_in['ln1_g'], 'L2_xattn_ln1_b': _L2_xattn_in['ln1_b'], 'L2_xattn_ln2_g': _L2_xattn_in['ln2_g'], 'L2_xattn_ln2_b': _L2_xattn_in['ln2_b'], 'L2_xattn_ln3_g': _L2_xattn_in['ln3_g'], 'L2_xattn_ln3_b': _L2_xattn_in['ln3_b'], 'L2_xattn_fc1_w': _L2_xattn_in['fc1_w'], 'L2_xattn_fc1_b': _L2_xattn_in['fc1_b'], 'L2_xattn_fc2_w': _L2_xattn_in['fc2_w'], 'L2_xattn_fc2_b': _L2_xattn_in['fc2_b'], 'L3_xattn_sa_wq': _L3_xattn_in['sa_wq'], 'L3_xattn_sa_wk': _L3_xattn_in['sa_wk'], 'L3_xattn_sa_wv': _L3_xattn_in['sa_wv'], 'L3_xattn_sa_wo': _L3_xattn_in['sa_wo'], 'L3_xattn_ca_wq': _L3_xattn_in['ca_wq'], 'L3_xattn_ca_wk': _L3_xattn_in['ca_wk'], 'L3_xattn_ca_wv': _L3_xattn_in['ca_wv'], 'L3_xattn_ca_wo': _L3_xattn_in['ca_wo'], 'L3_xattn_g_sa': _L3_xattn_in['g_sa'], 'L3_xattn_b_sa': _L3_xattn_in['b_sa'], 'L3_xattn_g_qca': _L3_xattn_in['g_qca'], 'L3_xattn_b_qca': _L3_xattn_in['b_qca'], 'L3_xattn_g_kca': _L3_xattn_in['g_kca'], 'L3_xattn_b_kca': _L3_xattn_in['b_kca'], 'L3_xattn_g_vca': _L3_xattn_in['g_vca'], 'L3_xattn_b_vca': _L3_xattn_in['b_vca'], 'L3_xattn_g_out': _L3_xattn_in['g_out'], 'L3_xattn_b_out': _L3_xattn_in['b_out'], 'L3_xattn_ffn_w1': _L3_xattn_in['ffn_w1'], 'L3_xattn_ffn_b1': _L3_xattn_in['ffn_b1'], 'L3_xattn_ffn_w2': _L3_xattn_in['ffn_w2'], 'L3_xattn_ffn_b2': _L3_xattn_in['ffn_b2']}

def reference(x, ctx_1024, mask_1x1xSxS2_ik0, mask_Bx1x1xS2_ik0, L0_xattn_Wq, L0_xattn_bq, L0_xattn_Wk, L0_xattn_bk, L0_xattn_Wv, L0_xattn_bv, L0_xattn_Wo, L0_xattn_bo, L0_xattn_gamma, L0_xattn_beta, L1_xattn_in_proj_w, L1_xattn_in_proj_b, L1_xattn_out_proj_w, L1_xattn_out_proj_b, L1_xattn_w1, L1_xattn_b1, L1_xattn_w2, L1_xattn_b2, L1_xattn_ln1_w, L1_xattn_ln1_b, L1_xattn_ln2_w, L1_xattn_ln2_b, L2_xattn_Wq1, L2_xattn_Wk1, L2_xattn_Wv1, L2_xattn_Wq2, L2_xattn_Wk2, L2_xattn_Wv2, L2_xattn_ln1_g, L2_xattn_ln1_b, L2_xattn_ln2_g, L2_xattn_ln2_b, L2_xattn_ln3_g, L2_xattn_ln3_b, L2_xattn_fc1_w, L2_xattn_fc1_b, L2_xattn_fc2_w, L2_xattn_fc2_b, L3_xattn_sa_wq, L3_xattn_sa_wk, L3_xattn_sa_wv, L3_xattn_sa_wo, L3_xattn_ca_wq, L3_xattn_ca_wk, L3_xattn_ca_wv, L3_xattn_ca_wo, L3_xattn_g_sa, L3_xattn_b_sa, L3_xattn_g_qca, L3_xattn_b_qca, L3_xattn_g_kca, L3_xattn_b_kca, L3_xattn_g_vca, L3_xattn_b_vca, L3_xattn_g_out, L3_xattn_b_out, L3_xattn_ffn_w1, L3_xattn_ffn_b1, L3_xattn_ffn_w2, L3_xattn_ffn_b2):
    import jax
    import jax.numpy as jnp

    def _L0_xattn_ref(q, k, v, attn_mask, pad_mask, Wq, bq, Wk, bk, Wv, bv, Wo, bo, gamma, beta):
        import jax, jax.numpy as jnp
        import numpy as np
        from math import sqrt
        B, S, D, H = (4, 512, 256, 16)
        HD = D // H

        def _mha(q, k, v, Wq, bq, Wk, bk, Wv, bv, Wo, bo, gamma, beta, attn_mask, pad_mask):
            seq = q.shape[1]
            x = jax.lax.stop_gradient(q)
            qp = (q @ Wq.T + bq).reshape(-1, H, seq, HD)
            kp = (k @ Wk.T + bk).reshape(-1, H, seq, HD)
            vp = (v @ Wv.T + bv).reshape(-1, H, seq, HD)
            scores = jnp.einsum('bhqd,bhkd->bhqk', qp, kp)
            scores = jnp.where(pad_mask == 0, -jnp.inf, scores)
            scores = jnp.where(attn_mask == 0, -jnp.inf, scores)
            attn = jax.nn.softmax(scores / sqrt(HD), axis=-1)
            out = jnp.einsum('bhqk,bhkd->bhqd', attn, vp).reshape(-1, seq, D)
            out = out @ Wo.T + bo
            y = x + out
            mean = jnp.mean(y, axis=-1, keepdims=True)
            std = jnp.sqrt(jnp.mean((y - mean) ** 2, axis=-1, keepdims=True))
            return gamma * ((y - mean) / (std + 1e-08)) + beta
        return _mha(q, k, v, Wq, bq, Wk, bk, Wv, bv, Wo, bo, gamma, beta, attn_mask, pad_mask)

    def _L1_xattn_ref(Q, K, V, in_proj_w, in_proj_b, out_proj_w, out_proj_b, w1, b1, w2, b2, ln1_w, ln1_b, ln2_w, ln2_b, num_heads):
        import jax, jax.numpy as jnp
        import numpy as np
        EPS = 1e-05

        def _layernorm(x, w, b):
            m = jnp.mean(x, axis=-1, keepdims=True)
            v = jnp.mean(jnp.square(x - m), axis=-1, keepdims=True)
            return (x - m) * jax.lax.rsqrt(v + EPS) * w + b
        B, S, E = Q.shape
        H = int(num_heads)
        d = E // H
        q = (Q @ in_proj_w[:E].T + in_proj_b[:E]).reshape(B, S, H, d)
        k = (K @ in_proj_w[E:2 * E].T + in_proj_b[E:2 * E]).reshape(B, S, H, d)
        v = (V @ in_proj_w[2 * E:].T + in_proj_b[2 * E:]).reshape(B, S, H, d)
        scores = jnp.einsum('bqhd,bkhd->bhqk', q, k) / jnp.sqrt(jnp.asarray(d, q.dtype))
        attn = jax.nn.softmax(scores, axis=-1)
        ctx = jnp.einsum('bhqk,bkhd->bqhd', attn, v).reshape(B, S, E)
        attn_out = ctx @ out_proj_w.T + out_proj_b
        x = _layernorm(Q + attn_out, ln1_w, ln1_b)
        ff = jnp.tanh(x @ w1.T + b1) @ w2.T + b2
        return _layernorm(x + ff, ln2_w, ln2_b)

    def _L2_xattn_ref(x, context, Wq1, Wk1, Wv1, Wq2, Wk2, Wv2, ln1_g, ln1_b, ln2_g, ln2_b, ln3_g, ln3_b, fc1_w, fc1_b, fc2_w, fc2_b):
        import jax, jax.numpy as jnp
        import numpy as np
        EPS = 1e-05

        def _layernorm(x, g, b):
            m = jnp.mean(x, axis=-1, keepdims=True)
            v = jnp.mean((x - m) ** 2, axis=-1, keepdims=True)
            return (x - m) / jnp.sqrt(v + EPS) * g + b

        def _mha(x, kv, Wq, Wk, Wv, mask, causal):
            m = mask[:, None]
            Q = jnp.einsum('bsd,hdk->bhsk', x, Wq) * m
            K = jnp.einsum('bsd,hdk->bhsk', kv, Wk) * m
            V = jnp.einsum('bsd,hdk->bhsk', kv, Wv) * m
            energy = jnp.einsum('bhsk,bhtk->bhst', Q, K)
            S = energy.shape[-1]
            lengths = jnp.sum(energy[:, :, 0, :] != 0, axis=-1)
            cols = jnp.arange(S)
            energy = jnp.where(cols[None, None, None, :] >= lengths[:, :, None, None], -jnp.inf, energy)
            if causal:
                energy = jnp.where(cols[None, :] > cols[:, None], -jnp.inf, energy)
            dk = Wq.shape[-1]
            score = jax.nn.softmax(energy / jnp.sqrt(jnp.asarray(dk, energy.dtype)), axis=-1)
            out = jnp.einsum('bhst,bhtk->bhsk', score, V) * m
            B, H, Sx, dkk = out.shape
            return out.transpose(0, 2, 1, 3).reshape(B, Sx, H * dkk)
        mask0 = 1.0 - jnp.all(x == 0, axis=2, keepdims=True).astype(x.dtype)
        z = _mha(x, x, Wq1, Wk1, Wv1, mask0, causal=True)
        x1 = _layernorm(x + z, ln1_g, ln1_b)
        mask1 = 1.0 - jnp.all(x1 == 0, axis=2, keepdims=True).astype(x1.dtype)
        z = _mha(x1, context, Wq2, Wk2, Wv2, mask1, causal=False)
        x2 = _layernorm(x1 + z, ln2_g, ln2_b)
        z = jnp.maximum(x2 @ fc1_w.T + fc1_b, 0.0) * mask0
        z = (z @ fc2_w.T + fc2_b) * mask0
        return _layernorm(x2 + z, ln3_g, ln3_b)

    def _L3_xattn_ref(q, k, v, sa_wq, sa_wk, sa_wv, sa_wo, ca_wq, ca_wk, ca_wv, ca_wo, g_sa, b_sa, g_qca, b_qca, g_kca, b_kca, g_vca, b_vca, g_out, b_out, ffn_w1, ffn_b1, ffn_w2, ffn_b2):
        import jax, jax.numpy as jnp
        import numpy as np
        D = 256
        H = 16
        DF = 4 * D
        LQ, LKV, B = (512, 1024, 2)
        EPS = 1e-05

        def _ln(x, g, b):
            mu = jnp.mean(x, axis=-1, keepdims=True)
            var = jnp.mean(jnp.square(x - mu), axis=-1, keepdims=True)
            return (x - mu) * jax.lax.rsqrt(var + EPS) * g + b

        def _mha(q, k, v, wq, wk, wv, wo):
            q = q @ wq.T
            k = k @ wk.T
            v = v @ wv.T
            b, lq, _ = q.shape
            lv = v.shape[1]
            qh = q.reshape(b, lq, H, -1).transpose(0, 2, 1, 3)
            kh = k.reshape(b, lv, H, -1).transpose(0, 2, 1, 3)
            vh = v.reshape(b, lv, H, -1).transpose(0, 2, 1, 3)
            dh = qh.shape[-1]
            scores = jnp.einsum('bhqd,bhkd->bhqk', qh, kh) / jnp.sqrt(jnp.float32(dh))
            attn = jax.nn.softmax(scores, axis=-1)
            o = jnp.einsum('bhqk,bhkd->bhqd', attn, vh)
            o = o.transpose(0, 2, 1, 3).reshape(b, lq, -1)
            return o @ wo.T
        q = _ln(q, g_sa, b_sa)
        q = q + _mha(q, q, q, sa_wq, sa_wk, sa_wv, sa_wo)
        q = _ln(q, g_qca, b_qca)
        k = _ln(k, g_kca, b_kca)
        v = _ln(v, g_vca, b_vca)
        q = q[..., :D] + _mha(q, k, v, ca_wq, ca_wk, ca_wv, ca_wo)
        h = _ln(q, g_out, b_out)
        h = jax.nn.relu(h @ ffn_w1.T + ffn_b1) @ ffn_w2.T + ffn_b2
        return q + h
    x = _L0_xattn_ref(x, ctx_1024, ctx_1024, mask_1x1xSxS2_ik0, mask_Bx1x1xS2_ik0, L0_xattn_Wq, L0_xattn_bq, L0_xattn_Wk, L0_xattn_bk, L0_xattn_Wv, L0_xattn_bv, L0_xattn_Wo, L0_xattn_bo, L0_xattn_gamma, L0_xattn_beta)
    x = _L1_xattn_ref(x, ctx_1024, ctx_1024, L1_xattn_in_proj_w, L1_xattn_in_proj_b, L1_xattn_out_proj_w, L1_xattn_out_proj_b, L1_xattn_w1, L1_xattn_b1, L1_xattn_w2, L1_xattn_b2, L1_xattn_ln1_w, L1_xattn_ln1_b, L1_xattn_ln2_w, L1_xattn_ln2_b, 16)
    x = _L2_xattn_ref(x, ctx_1024, L2_xattn_Wq1, L2_xattn_Wk1, L2_xattn_Wv1, L2_xattn_Wq2, L2_xattn_Wk2, L2_xattn_Wv2, L2_xattn_ln1_g, L2_xattn_ln1_b, L2_xattn_ln2_g, L2_xattn_ln2_b, L2_xattn_ln3_g, L2_xattn_ln3_b, L2_xattn_fc1_w, L2_xattn_fc1_b, L2_xattn_fc2_w, L2_xattn_fc2_b)
    x = _L3_xattn_ref(x, ctx_1024, ctx_1024, L3_xattn_sa_wq, L3_xattn_sa_wk, L3_xattn_sa_wv, L3_xattn_sa_wo, L3_xattn_ca_wq, L3_xattn_ca_wk, L3_xattn_ca_wv, L3_xattn_ca_wo, L3_xattn_g_sa, L3_xattn_b_sa, L3_xattn_g_qca, L3_xattn_b_qca, L3_xattn_g_kca, L3_xattn_b_kca, L3_xattn_g_vca, L3_xattn_b_vca, L3_xattn_g_out, L3_xattn_b_out, L3_xattn_ffn_w1, L3_xattn_ffn_b1, L3_xattn_ffn_w2, L3_xattn_ffn_b2)
    return x

_drawn_inputs = setup_inputs


def setup_inputs(seed=0):
    import zlib

    import numpy as np

    out = dict(_drawn_inputs(seed))
    spreads = {'L0_xattn_bq': (0.0, 0.8),
     'L0_xattn_bk': (0.0, 0.8),
     'L0_xattn_bv': (0.0, 0.8),
     'L0_xattn_bo': (0.0, 0.1),
     'L0_xattn_gamma': (1.0, 0.2),
     'L0_xattn_beta': (0.0, 0.1),
     'L1_xattn_ln1_w': (1.0, 0.2),
     'L1_xattn_ln1_b': (0.0, 0.1),
     'L1_xattn_ln2_w': (1.0, 0.2),
     'L1_xattn_ln2_b': (0.0, 0.1),
     'L2_xattn_ln1_g': (1.0, 0.2),
     'L2_xattn_ln1_b': (0.0, 0.1),
     'L2_xattn_ln2_g': (1.0, 0.2),
     'L2_xattn_ln2_b': (0.0, 0.1),
     'L2_xattn_ln3_g': (1.0, 0.2),
     'L2_xattn_ln3_b': (0.0, 0.1),
     'L2_xattn_fc1_b': (0.0, 0.377),
     'L2_xattn_fc2_b': (0.0, 0.1),
     'L3_xattn_g_sa': (1.0, 0.2),
     'L3_xattn_b_sa': (0.0, 0.1),
     'L3_xattn_g_qca': (1.0, 0.2),
     'L3_xattn_b_qca': (0.0, 0.1),
     'L3_xattn_g_kca': (1.0, 0.6),
     'L3_xattn_b_kca': (0.0, 0.8),
     'L3_xattn_g_vca': (1.0, 0.6),
     'L3_xattn_b_vca': (0.0, 0.747),
     'L3_xattn_g_out': (1.0, 0.2),
     'L3_xattn_b_out': (0.0, 0.56),
     'L3_xattn_ffn_b1': (0.0, 0.1),
     'L3_xattn_ffn_b2': (0.0, 0.1)}
    factors = {'L0_xattn_Wq': 8.0,
     'L0_xattn_Wk': 8.0,
     'L1_xattn_in_proj_b': 8.0,
     'L1_xattn_out_proj_b': 2.979,
     'L1_xattn_b1': 4.914,
     'L1_xattn_b2': 3.02,
     'L2_xattn_Wq1': 8.0,
     'L2_xattn_Wk1': 8.0,
     'L2_xattn_Wq2': 8.0,
     'L2_xattn_Wk2': 8.0,
     'L3_xattn_sa_wq': 8.0,
     'L3_xattn_sa_wk': 8.0,
     'L3_xattn_ca_wq': 8.0,
     'L3_xattn_ca_wk': 8.0}
    for name, (base, spread) in spreads.items():
        noise = np.random.default_rng([zlib.crc32(name.encode()), seed]).standard_normal(out[name].shape)
        drawn = base * np.exp(spread * noise) if base else spread * noise
        out[name] = jnp.asarray(drawn.astype(out[name].dtype))
    for name, factor in factors.items():
        out[name] = (out[name] * factor).astype(out[name].dtype)
    return out
```

```python
from contextlib import ExitStack

import numpy as np

import concourse.bass as bass
from concourse import mybir

P = 128
B, S, D, H = 16, 256, 256, 16
HD = D // H
DF = 4 * D
NB = 4
ITERS = B // NB
NA = 6
NU = NA * NB
SCALE = float(HD) ** -0.5
NEG = -1.0e30
FLOOR = -1.0e28
EPS = 1e-5
ROWS = 6 * HD
PEN, SHIFT = ROWS, ROWS + 1
PT_SLOTS = 6
NO_PEN = 32

F32 = mybir.dt.float32
BF16 = mybir.dt.bfloat16
I32 = mybir.dt.int32
ALU = mybir.AluOpType
ACT = mybir.ActivationFunctionType
AX = mybir.AxisListType.X

WEIGHTS = [("q0", 512), ("k0", 512), ("v0", 512), ("o0", 1024),
           ("q1", 512), ("k1", 512), ("v1", 512), ("o1", 512), ("u1", 2048), ("d1", 2048),
           ("q2", 512), ("k2", 512), ("v2", 512), ("q3", 512), ("k3", 512), ("v3", 512), ("u3", 512), ("d3", 512),
           ("q4", 512), ("k4", 512), ("v4", 512), ("o4", 512), ("q5", 512), ("k5", 512), ("v5", 512), ("o5", 512),
           ("u5", 2048), ("d5", 2048)]
WOFF, WCOLS = {}, 0
for _name, _n in WEIGHTS:
    WOFF[_name] = WCOLS
    WCOLS += _n
W_PARTS = [(0, WOFF["q1"]), (WOFF["q1"], WOFF["q2"]), (WOFF["q2"], WCOLS)]
TILES = ["v0", "o0", "g0", "b0", "v1", "o1", "g10", "b10", "d1", "g11", "b11", "g20", "b20", "g30", "b30",
         "g31", "b31", "d3", "g32", "b32", "g40", "b40", "d5"]
COLS = [("qk0", 16), ("q1", 2), ("k1", 2), ("u1", 8), ("u3", 2), ("u5", 8),
        ("gk", 2), ("bk", 2), ("gv", 2), ("bv", 2), ("gh", 2), ("bh", 2)]
COFF, NCOLS = {}, 0
for _name, _n in COLS:
    COFF[_name] = NCOLS
    NCOLS += _n

POST = {
    0: [("pb", 0, 0), ("otr", 0, 2), ("otr", 1, 3), ("ott", 0, 6), ("opr", 0, 7), ("lnA", 0, 8), ("lnB", 0, 9),
        ("xtr", 0, 13)],
    1: [("pb", 0, 0), ("otr", 0, 2), ("otr", 1, 3), ("ott", 0, 4), ("opr", 0, 5), ("lnA", 0, 6), ("lnB", 0, 7),
        ("xtr", 0, 11), ("pb", 1, 12), ("ff1", 0, 12), ("ff1", 1, 13), ("ff1", 2, 14), ("ff1", 3, 15),
        ("ff2", 0, 16), ("ff2", 1, 17), ("lnA", 1, 18), ("lnB", 1, 19), ("xtr", 1, 22), ("msk", 0, 23)],
    2: [("otr", 0, 2), ("otr", 1, 3), ("res", 0, 4), ("lnA", 0, 5), ("lnB", 0, 6), ("xtr", 0, 10), ("msk", 0, 11)],
    3: [("otr", 0, 2), ("otr", 1, 3), ("res", 0, 4), ("lnA", 0, 5), ("lnB", 0, 6), ("xtr", 0, 10), ("ff1", 0, 11),
        ("ff2", 0, 13), ("ff2", 1, 14), ("lnA", 1, 15), ("lnB", 1, 16), ("lnA", 2, 18), ("lnB", 2, 19),
        ("xtr", 1, 22)],
    4: [("otr", 0, 2), ("otr", 1, 3), ("ott", 0, 4), ("opr", 0, 5), ("lnA", 0, 6), ("lnB", 0, 7), ("xtr", 0, 11)],
    5: [("otr", 0, 2), ("otr", 1, 3), ("ott", 0, 4), ("opr", 0, 5), ("lnA", 0, 6), ("lnB", 0, 7), ("pb", 0, 8),
        ("xtr", 0, 9), ("ff1", 0, 10), ("ff1", 1, 11), ("ff1", 2, 12), ("ff1", 3, 13), ("ff2", 0, 14), ("ff2", 1, 15),
        ("store", 0, 16)],
}


def pre(a):
    out = []
    if a != 2 and a != 4:
        out.append(("load", 0, 0))
    if a == 3:
        out.append(("ctr", 0, 3))
    if a == 5:
        out += [("clnA", 0, 1), ("clnB", 0, 2), ("ctr", 0, 3)]
    out += [("pqk", 0, 7), ("pqk", 1, 8)]
    if a in (2, 3):
        out += [("e0", 0, 8), ("len", 0, 10)]
    out += [("hi", 0, 9), ("hi", 1, 9), ("mid", 0, 11), ("mid", 1, 11), ("swr", 0, 11), ("swr", 1, 12), ("srd", 0, 13), ("srd", 1, 17),
            ("pvv", 0, 18)]
    if a == 0:
        out += [("pvt", 0, 20), ("pvt", 1, 21)]
    return out


def plan():
    slots = {}
    for n in range(NU):
        a = n // NB
        for kind, i, at in POST[a]:
            slots.setdefault((n + 2) * 16 + at, []).append((kind, n, i))
    for n in range(NU):
        for kind, i, at in pre(n // NB):
            slots.setdefault((n - 1) * 16 + at, []).append((kind, n, i))
    for n in range(NU):
        for s in range(16):
            slots.setdefault(n * 16 + s, []).append(("nat", n, s))
        for half in range(2):
            slots[n * 16 + 8 * half + 7].append(("neg", n, half))
            slots.setdefault(n * 16 + 8 * half + 9, []).insert(0, ("nmt", n, half))
    for n in range(NU):
        for s in range(16):
            slots.setdefault((n + 1) * 16 + s, []).append(("st", n, s))
        for g in range(4):
            slots.setdefault((n + 1) * 16 + 4 * g + 5, []).append(("pvg", n, g))
            if g % 2:
                slots[(n + 1) * 16 + 4 * g + 5].append(("pvout", n, g // 2))
    return [e for at in sorted(slots) for e in slots[at]]


ORDER = plan()
NTH, _seen = {}, {}
for _e in ORDER:
    _seen[_e[0]] = _seen.get(_e[0], 0) + 1
    NTH[_e] = _seen[_e[0]]
FF3_BEFORE = {n: sum(e[0] == "ff2" and e[1] // NB == 3 for e in ORDER[:ORDER.index(("len", n, 0))])
              for n in range(2 * NB, 4 * NB)}
_ln = [(e[1], e[2]) for e in ORDER if e[0] == "lnB" and e[1] < 5 * NB]
LN_DONE = {e: k + 1 for k, e in enumerate(_ln)}
MISC_KINDS = ("nmt", "pqk", "pvv", "pvt", "ctr", "e0", "otr", "ott", "opr", "xtr", "ff1", "ff2")
MISC, _used = {}, 0
for _e in ORDER:
    if _e[0] in MISC_KINDS and not (_e[0] == "ott" and _e[1] < NB):
        MISC[_e] = (_used % 2, _used // 2 + 1)
        _used += 1


def block_kernel(nc, t):
    with ExitStack() as ctx:
        def sb(name, shape, dt=F32):
            return ctx.enter_context(nc.sbuf_tensor(name, shape, dt))

        sems = []

        def sem(name):
            s = ctx.enter_context(nc.semaphore(name))
            sems.append(s)
            return s

        weights = sb("weights", [P, WCOLS])
        tiles = sb("tiles", [P, len(TILES), D])
        cols = sb("cols", [P, NCOLS])
        ident = sb("ident", [P, P])
        ident_b = sb("ident_b", [P, P], BF16)
        mask0 = sb("mask0", [P, 2, S], BF16)
        mask0_t = sb("mask0_t", [P, 2, S], BF16)
        causal = sb("causal", [P, 2, S], BF16)
        causal_t = sb("causal_t", [P, 2, S], BF16)
        headsel = sb("headsel", [P, 2, H])
        iota = sb("iota", [H, S])
        half_pow = sb("half_pow", [P, 2, 2])
        xn = sb("xn", [P, NB, 2, D])
        xT = sb("xT", [P, 2, 2, S])
        cT = sb("cT", [P, 2, 2, S])
        vT = sb("vT", [P, 2, S])
        cn = sb("cn", [P, 2, D])
        tmask = sb("tmask", [P, NB, 2, 2])
        pad_i = sb("pad_i", [NB, S], I32)
        pen_row = sb("pen_row", [NO_PEN + 1, S], BF16)
        xb = sb("xb", [P, 2, 512])
        parts = sb("parts", [P, 2, 3, 512], BF16)
        qst = sb("qst", [P, 2, H, S], BF16)
        kst = sb("kst", [P, 2, H, S], BF16)
        vaug = sb("vaug", [P, 2, 2, H, 32])
        vflip = sb("vflip", [P, 2, 512])
        q0blk = sb("q0blk", [P, 2, H])
        length = sb("length", [H, 1])
        pen16 = sb("pen16", [H, 2, S], BF16)
        mraw = sb("mraw", [P, 2, 2, 8])
        negm = sb("negm", [P, 2, 16])
        negm_t = sb("negm_t", [16, 2, P], BF16)
        pt = sb("pt", [P, PT_SLOTS, 2, S])
        ote = sb("ote", [P, 2, 2, S])
        rec = sb("rec", [P, 2, H])
        on = sb("on", [P, 2, D])
        on0 = sb("on0", [P, 2, H, 32])
        ot = sb("ot", [P, 2, S])
        ot0 = vflip
        stats = sb("stats", [P, NB + 1, 2, 6])
        mv = sb("mv", [P, NB + 1, 2, 2])
        var = sb("var", [P, NB + 1, 2])
        rstd = sb("rstd", [P, NB + 1, 2])
        hbuf = cn
        hT = sb("hT", [P, 8, S])
        zt = sb("zt", [P, D])
        nonzero = zt[0:H, :]

        ps_nat = ctx.enter_context(nc.psum_tensor("ps_nat", [P, 2, 2, S], F32))
        ps_st = ctx.enter_context(nc.psum_tensor("ps_st", [P, 2, 2, S], F32))
        ps_pv = ctx.enter_context(nc.psum_tensor("ps_pv", [P, 2, 2, S], F32))
        ps_misc = ctx.enter_context(nc.psum_tensor("ps_misc", [P, 2, 512], F32))

        w_loaded = [ctx.enter_context(nc.semaphore(f"w_loaded{i}")) for i in range(len(W_PARTS))]
        const_loaded = ctx.enter_context(nc.semaphore("const_loaded"))
        const_made = ctx.enter_context(nc.semaphore("const_made"))
        fill_done = ctx.enter_context(nc.semaphore("fill_done"))
        raw_masks = ctx.enter_context(nc.semaphore("raw_masks"))

        pad_loaded, pad_made = sem("pad_loaded"), sem("pad_made")
        x_loaded = [sem(f"x_loaded{u}") for u in range(NB)]
        xT_loaded = [sem(f"xT_loaded{r}") for r in range(2)]
        cT_loaded = [sem(f"cT_loaded{r}") for r in range(2)]
        cn_loaded, cmask_done = sem("cn_loaded"), sem("cmask_done")
        cln_var, cln_rstd, cln_hat = sem("cln_var"), sem("cln_rstd"), sem("cln_hat")
        misc_ready = [sem(f"misc_ready{b}") for b in range(2)]
        misc_out = [sem(f"misc_out{b}") for b in range(2)]
        xb_biased = sem("xb_biased")
        hi_done, rest_done, mid_done, lo_done = sem("hi_done"), sem("rest_done"), sem("mid_done"), sem("lo_done")
        q0_ready, pen_ready = sem("q0_ready"), sem("pen_ready")
        scr_written = [[sem(f"scr_written{r}{c}") for c in range(2)] for r in range(2)]
        stack_ready = [[sem(f"stack_ready{r}{h}") for h in range(2)] for r in range(2)]
        shift_ready = [[sem(f"shift_ready{r}{h}") for h in range(2)] for r in range(2)]
        v_flipped = sem("v_flipped")
        nat_done, max_done, neg_done = sem("nat_done"), sem("max_done"), sem("neg_done")
        st_done, exp_done, pv_done, ote_ready = sem("st_done"), sem("exp_done"), sem("pv_done"), sem("ote_ready")
        ot0_ready = sem("ot0_ready")
        res_done, bias_done = sem("res_done"), sem("bias_done")
        ln_var, ln_rstd, ln_hat, ln_done = sem("ln_var"), sem("ln_rstd"), sem("ln_hat"), sem("ln_done")
        ff3_done, msk_done = sem("ff3_done"), sem("msk_done")
        stored = sem("stored")
        dve_link, pool_link = sem("dve_link"), sem("pool_link")
        group_sems = range(min(s.num for s in sems), max(s.num for s in sems) + 1)
        assert len(group_sems) == len(sems)

        def w(name, *dims):
            n = dict(WEIGHTS)[name]
            v = weights[:, WOFF[name]:WOFF[name] + n]
            return v.rearrange("p (a b) -> p a b", b=dims[0])

        def tile(name):
            return tiles[:, TILES.index(name), :]

        def tile2(name):
            return tiles[:, TILES.index(name), :].unsqueeze(1).to_broadcast([P, 2, D])

        def col(name, i):
            return cols[:, COFF[name] + i:COFF[name] + i + 1]

        def parity(n, per=1):
            return (n // 2 + 1) * per

        def wait_out(eng, e):
            bank, k = MISC[e]
            eng.wait_ge(misc_out[bank], k)

        def wait_filled(eng, e):
            bank, k = MISC[e]
            eng.wait_ge(misc_ready[bank], k)

        def written(n):
            return sum(8 if m < NB else 1 for m in range(n % 2, n + 1, 2))

        scr = t["scratch"]

        with nc.Block() as block:
            @block.sync
            def _(sp):
                for name, dst in (("cols", cols), ("ident", ident), ("headsel", headsel), ("iota", iota),
                                  ("half_pow", half_pow)):
                    sp.dma_start(dst[:], t[name]).then_inc(const_loaded, 16)
                sp.dma_start(xb[:, 0, :].bitcast(I32), t["attn"][:, 0]).then_inc(raw_masks, 16)
                sp.dma_start(xb[:, 1, :].bitcast(I32), t["attn"][:, 1]).then_inc(raw_masks, 16)
                sp.dma_start(ot0[:, :, :], t["causal"]).then_inc(raw_masks, 16)
                sp.dma_start(tiles[:], t["tiles"].partition_broadcast(P)).then_inc(const_loaded, 16)
                for i, (lo, hi) in enumerate(W_PARTS):
                    sp.dma_start(weights[:, lo:hi], t["weights"][:, lo:hi]).then_inc(w_loaded[i], 16)
                sp.wait_ge(const_loaded, 96)

            @block.vector
            def _(dve):
                dve.wait_ge(raw_masks, 48)
                nc.vector.tensor_scalar(mask0[:].rearrange("p a b -> p (a b)"), xb[:, 0, :].bitcast(I32), 0.0, NEG,
                                        ALU.is_equal, ALU.mult).then_inc(const_made, 1)
                nc.vector.tensor_scalar(mask0_t[:].rearrange("p a b -> p (a b)"), xb[:, 1, :].bitcast(I32), 0.0, NEG,
                                        ALU.is_equal, ALU.mult).then_inc(const_made, 1)
                nc.vector.tensor_scalar(causal[:].rearrange("p a b -> p (a b)"), ot0[:, 0, :], NEG, None,
                                        ALU.mult).then_inc(const_made, 1)
                nc.vector.tensor_scalar(causal_t[:].rearrange("p a b -> p (a b)"), ot0[:, 1, :], NEG, None,
                                        ALU.mult).then_inc(const_made, 1)
                dve.wait_ge(const_loaded, 96)
                nc.vector.tensor_copy(ident_b[:], ident[:]).then_inc(const_made, 1)

            @block.gpsimd
            def _(pool):
                nc.gpsimd.memset(qst[PEN:PEN + 2], 1.0).then_inc(fill_done, 1)
                pool.wait_ge(fill_done, 1)
                nc.gpsimd.memset(kst[PEN:PEN + 2], 1.0).then_inc(fill_done, 1)
                pool.wait_ge(fill_done, 2)
                nc.gpsimd.memset(vaug[:], 0.0).then_inc(fill_done, 1)
                pool.wait_ge(fill_done, 3)
                nc.gpsimd.memset(on0[:], 0.0).then_inc(fill_done, 1)
                pool.wait_ge(fill_done, 4)
                nc.gpsimd.memset(pen_row[NO_PEN:NO_PEN + 1, :], 0.0).then_inc(fill_done, 1)
                pool.wait_ge(fill_done, 5)
                nc.gpsimd.memset(vaug[:, :, :, :, HD:HD + 1].rearrange("p a b c d -> p (a b c) d"), 1.0).then_inc(fill_done, 1)
                pool.wait_ge(fill_done, 6)

        nc.all_engine_barrier()

        with nc.Fori(0, ITERS) as it:
            with nc.Block() as block:

                @block.sync
                def _(sp):
                    sp.dma_start(pad_i[:], t["pad"][it]).then_inc(pad_loaded, 16)
                    for e in ORDER:
                        kind, n, i = e
                        a, u, rot = n // NB, n % NB, n % 2
                        if kind == "load":
                            if a <= 1:
                                if n >= 2:
                                    wait_filled(sp, ("pvv", n - 2, 0))
                                sp.dma_start(cT[:, rot], t["ctx_t"][it, u]).then_inc(cT_loaded[rot], 16)
                            if a == 0:
                                if n >= 2:
                                    wait_filled(sp, ("pqk", n - 2, 1))
                                sp.dma_start(xT[:, rot], t["x_t"][it, u]).then_inc(xT_loaded[rot], 16)
                                sp.dma_start(xn[:, u], t["x"][it, u]).then_inc(x_loaded[u], 16)
                            if a in (3, 5):
                                if u > 0:
                                    wait_filled(sp, ("ctr", n - 1, 0))
                                elif a == 5:
                                    wait_filled(sp, ("ctr", 4 * NB - 1, 0))
                                sp.dma_start(cn[:], t["ctx"][it, u]).then_inc(cn_loaded, 16)
                        elif kind == "swr":
                            sp.wait_ge(lo_done, NTH["mid", n, i])
                            if n >= 2:
                                for half in range(2):
                                    sp.wait_ge(stack_ready[rot][half], parity(n - 2, 112))
                            if a == 0:
                                for pb in range(4):
                                    for qk in range(2):
                                        r = 32 * pb + 16 * qk
                                        s0 = i * 8 + pb * 2
                                        sp.dma_start(scr[rot, qk, :, :, s0:s0 + 2, :].rearrange("i d s t -> d i (s t)"),
                                                     parts[r:r + 16, i]).then_inc(scr_written[rot][i], 16)
                            else:
                                sp.dma_start(scr[rot, i].rearrange("i d (h a) t -> (d h) i (a t)", a=2),
                                             parts[:, i]).then_inc(scr_written[rot][i], 16)
                        elif kind == "srd":
                            if n >= 2:
                                sp.wait_ge(st_done, NTH["st", n - 2, 8 * i + 7])
                            for c in range(2):
                                sp.wait_ge(scr_written[rot][c], 16 * written(n))
                            sl = slice(8 * i, 8 * i + 8)

                            def put(dst, row, qk, p0, np_):
                                src = scr[rot, qk, p0:p0 + np_, :, sl, :].rearrange("i d s t -> (i d) (s t)")
                                sp.dma_start(dst[row:row + 16 * np_, rot, sl, :], src).then_inc(stack_ready[rot][i], 16)

                            put(qst, 0, 0, 0, 3)
                            put(qst, 48, 0, 0, 2)
                            put(qst, 80, 0, 0, 1)
                            for row, copies, p0 in ((0, 3, 0), (48, 2, 1), (80, 1, 2)):
                                src = scr[rot, 1, p0, :, sl, :].rearrange("d s t -> d (s t)")
                                if copies > 1:
                                    src = src.partition_broadcast(copies)
                                sp.dma_start(kst[row:row + 16 * copies, rot, sl, :], src).then_inc(stack_ready[rot][i], 16)
                            if a in (2, 3):
                                sp.wait_ge(pen_ready, NTH["e0", n, 0])
                                src = pen16[8 * i:8 * i + 8, rot, :]
                            else:
                                if a == 0 and i == 0:
                                    sp.wait_ge(pad_made, 1)
                                k = u if a == 0 else NO_PEN
                                src = pen_row[k:k + 1, :].unsqueeze(1).to_broadcast([1, 8, S])
                            sp.dma_start(kst[PEN:PEN + 1, rot, sl, :], src).then_inc(stack_ready[rot][i], 16)
                        elif kind == "nmt":
                            wait_out(sp, e)
                            for qh in range(2):
                                sp.dma_start(qst[SHIFT:SHIFT + 1, rot, 8 * i:8 * i + 8, qh * P:(qh + 1) * P],
                                             negm_t[8 * qh:8 * qh + 8, i, :]).then_inc(shift_ready[rot][i], 16)
                        elif kind == "store":
                            wait_out(sp, ("ff2", n, 1))
                            sp.dma_start(t["out"][it, u], xn[:, u]).then_inc(stored, 16)
                    sp.wait_ge(stored, 16 * NB)

                @block.tensor
                def _(pe):
                    def open_bank(e):
                        bank, k = MISC[e]
                        if k > 1:
                            pe.wait_ge(misc_out[bank], k - 1)
                        return ps_misc[:, bank, :]

                    def filled(e, last):
                        last.then_inc(misc_ready[MISC[e][0]], 1)

                    def need_xT(n):
                        a, u = n // NB, n % NB
                        if a == 0:
                            pe.wait_ge(xT_loaded[n % 2], 16 * parity(n))
                        else:
                            wait_out(pe, ("xtr", n - NB, 1 if a in (2, 4) else 0))

                    def need_cT(n):
                        if n // NB <= 1:
                            pe.wait_ge(cT_loaded[n % 2], 16 * parity(n))
                        else:
                            wait_out(pe, ("ctr", n, 0))

                    pe.wait_ge(w_loaded[0], 16)
                    for e in ORDER:
                        kind, n, i = e
                        a, u, rot = n // NB, n % NB, n % 2
                        src_x, src_c = xT[:, u % 2], cT[:, rot]
                        if kind == "pqk":
                            need_xT(n)
                            if a not in (2, 4):
                                need_cT(n)
                            if a == 1:
                                pe.wait_ge(w_loaded[1], 16)
                            if a == 2:
                                pe.wait_ge(w_loaded[2], 16)
                            bank = open_bank(e)
                            if a == 0:
                                out = bank.rearrange("p (c w) -> p c w", w=32)
                                for qk, src in enumerate((src_x, src_c)):
                                    for dk in range(2):
                                        last = nc.tensor.matmul(out[:, :, 16 * qk:16 * qk + 16],
                                                                src[:, dk, i * P:(i + 1) * P], w("qk"[qk] + "0", D)[:, dk, :],
                                                                start=dk == 0, stop=dk == 1)
                            else:
                                src = src_x if i == 0 or a in (2, 4) else src_c
                                wv = w("qk"[i] + str(a), P)
                                for a2 in range(2):
                                    for dk in range(2):
                                        last = nc.tensor.matmul(bank[:, a2 * S:(a2 + 1) * S], wv[:, 2 * dk + a2, :],
                                                                src[:, dk, :], start=dk == 0, stop=dk == 1)
                            filled(e, last)
                        elif kind == "e0":
                            pe.wait_ge(q0_ready, NTH[e])
                            wait_out(pe, ("pqk", n, 1))
                            bank = open_bank(e)
                            for a2 in range(2):
                                last = nc.tensor.matmul(bank[0:H, 0:S], q0blk[:, a2, :], xb[:, 1, a2 * S:(a2 + 1) * S],
                                                        start=a2 == 0, stop=a2 == 1)
                            filled(e, last)
                        elif kind == "pvv":
                            src = src_x if a in (2, 4) else vT[:] if a == 5 else src_c
                            bank = open_bank(e)
                            wv = w("v" + str(a), D)
                            for hf in range(2):
                                for dk in range(2):
                                    last = nc.tensor.matmul(bank[:, hf * D:(hf + 1) * D], src[:, dk, hf * P:(hf + 1) * P],
                                                            wv[:, dk, :], start=dk == 0, stop=dk == 1)
                            filled(e, last)
                        elif kind == "pvt":
                            pe.wait_ge(v_flipped, n + 1)
                            bank = open_bank(e)
                            for hf in range(2):
                                v = vflip[:, hf, :].rearrange("p (h k) -> p h k", h=2)
                                for h2 in range(2):
                                    k = 2 * hf + h2
                                    last = nc.tensor.transpose(bank[:, k * P:(k + 1) * P], v[:, h2, i * P:(i + 1) * P], ident[:])
                            filled(e, last)
                        elif kind == "ctr":
                            if a == 3:
                                pe.wait_ge(cmask_done, u + 1)
                            else:
                                pe.wait_ge(cln_hat, u + 1)
                            bank = open_bank(e)
                            for dk in range(2):
                                for hf in range(2):
                                    k = 2 * dk + hf
                                    last = nc.tensor.transpose(bank[:, k * P:(k + 1) * P], cn[:, hf, dk * P:(dk + 1) * P], ident[:])
                            filled(e, last)
                        elif kind == "nat":
                            if i % 8 == 0:
                                pe.wait_ge(stack_ready[rot][i // 8], parity(n, 112))
                            k = NTH[e]
                            if k > 2:
                                pe.wait_ge(max_done, k - 2)
                            mask = {0: mask0, 2: causal}.get(a)
                            for hf in range(2):
                                out = ps_nat[:, i % 2, hf, :]
                                last = nc.tensor.matmul(out, qst[0:PEN + 1, rot, i, hf * P:(hf + 1) * P],
                                                        kst[0:PEN + 1, rot, i, :], start=True, stop=mask is None)
                                if mask is not None:
                                    last = nc.tensor.matmul(out, ident_b[:], mask[:, hf, :], start=False, stop=True)
                            last.then_inc(nat_done, 1)
                        elif kind == "nmt":
                            pe.wait_ge(neg_done, NTH[e])
                            bank = open_bank(e)
                            filled(e, nc.tensor.transpose(bank[0:16, 0:P], negm[:, i, :], ident[:]))
                        elif kind == "st":
                            if i % 8 == 0:
                                pe.wait_ge(shift_ready[rot][i // 8], parity(n, 32))
                            k = NTH[e]
                            if k > 2:
                                pe.wait_ge(exp_done, k - 2)
                            mask = {0: mask0_t, 2: causal_t}.get(a)
                            for kh in range(2):
                                out = ps_st[:, i % 2, kh, :]
                                last = nc.tensor.matmul(out, kst[0:SHIFT + 1, rot, i, kh * P:(kh + 1) * P],
                                                        qst[0:SHIFT + 1, rot, i, :], start=True, stop=mask is None)
                                if mask is not None:
                                    last = nc.tensor.matmul(out, ident_b[:], mask[:, kh, :], start=False, stop=True)
                            last.then_inc(st_done, 1)
                        elif kind == "pvg":
                            pe.wait_ge(exp_done, NTH["st", n, 4 * i + 3])
                            if i == 0:
                                wait_out(pe, ("pvt", n, 1) if a == 0 else ("pvv", n, 0))
                                if a == 0:
                                    wait_out(pe, ("pvt", n, 0))
                            if i % 2 == 0 and n > 0:
                                pe.wait_ge(ote_ready, NTH["pvout", n - 1, i // 2])
                            for kh in range(2):
                                for j in range(4):
                                    s = 4 * i + j
                                    last = nc.tensor.matmul(ps_pv[32 * j:32 * j + 32, i // 2, i % 2, :], vaug[:, rot, kh, s, :],
                                                            pt[:, (n * H + s) % PT_SLOTS, kh, :], start=kh == 0, stop=kh == 1)
                            last.then_inc(pv_done, 1)
                        elif kind == "otr":
                            pe.wait_ge(ote_ready, NTH["pvout", n, 1])
                            bank = open_bank(e)
                            for g in range(4):
                                last = nc.tensor.transpose(bank[:, g * P:(g + 1) * P], ote[:, g // 2, g % 2, i * P:(i + 1) * P], ident[:])
                            filled(e, last)
                        elif kind == "ott" and a > 0:
                            wait_out(pe, ("otr", n, 0))
                            wait_out(pe, ("otr", n, 1))
                            bank = open_bank(e)
                            for ch in range(2):
                                for hf in range(2):
                                    k = 2 * ch + hf
                                    last = nc.tensor.transpose(bank[:, k * P:(k + 1) * P], on[:, hf, ch * P:(ch + 1) * P], ident[:])
                            filled(e, last)
                        elif kind == "opr":
                            if a == 0:
                                pe.wait_ge(ot0_ready, n + 1)
                            else:
                                wait_out(pe, ("ott", n, 0))
                            bank = open_bank(e)
                            wo = w("o" + str(a), D)
                            for th in range(2):
                                for k in range(4 if a == 0 else 2):
                                    if a == 0:
                                        v = ot0[:, k // 2, :].rearrange("p (c s) -> p c s", c=2)
                                        lhs = v[:, k % 2, th * P:(th + 1) * P]
                                    else:
                                        lhs = ot[:, k, th * P:(th + 1) * P]
                                    last = nc.tensor.matmul(bank[:, th * D:(th + 1) * D], lhs, wo[:, k, :],
                                                            start=k == 0, stop=k == (3 if a == 0 else 1))
                            filled(e, last)
                        elif kind == "xtr":
                            if a == 5:
                                pe.wait_ge(ln_hat, NTH["lnB", n, 0])
                                src = hbuf[:]
                            else:
                                pe.wait_ge(ln_done, LN_DONE[n, 2 if a == 3 and i == 1 else i])
                                src = xn[:, u]
                            bank = open_bank(e)
                            for dk in range(2):
                                for hf in range(2):
                                    k = 2 * dk + hf
                                    last = nc.tensor.transpose(bank[:, k * P:(k + 1) * P], src[:, hf, dk * P:(dk + 1) * P], ident[:])
                            filled(e, last)
                        elif kind == "ff1":
                            if i == 0:
                                wait_out(pe, ("xtr", n, 0))
                            bank = open_bank(e)
                            wu = w("u" + str(a), D if a == 3 else DF)
                            for c in range(2):
                                ch = 2 * i + c
                                for dk in range(2):
                                    last = nc.tensor.matmul(bank[:, c * S:(c + 1) * S], wu[:, dk, ch * P:(ch + 1) * P],
                                                            src_x[:, dk, :], start=dk == 0, stop=dk == 1)
                            filled(e, last)
                        elif kind == "ff2":
                            nch = 2 if a == 3 else 8
                            for j in range(nch // 2):
                                wait_out(pe, ("ff1", n, j))
                            bank = open_bank(e)
                            wd = w("d" + str(a), D)
                            for ch in range(nch):
                                last = nc.tensor.matmul(bank[:, 0:D], hT[:, ch, i * P:(i + 1) * P], wd[:, ch, :],
                                                        start=ch == 0, stop=ch == nch - 1)
                            filled(e, last)

                @block.scalar
                def _(act):
                    def read_bank(e):
                        wait_filled(act, e)
                        return ps_misc[:, MISC[e][0], :]

                    def out_of_bank(e, last):
                        last.then_inc(misc_out[MISC[e][0]], 1)

                    for e in ORDER:
                        kind, n, i = e
                        a, u, rot = n // NB, n % NB, n % 2
                        if kind == "pqk" and a > 0:
                            bank = read_bank(e)
                            act.wait_ge(lo_done, NTH["mid", n - 1, i])
                            if a == 1:
                                for a2 in range(2):
                                    last = nc.scalar.activation(xb[:, i, a2 * S:(a2 + 1) * S], bank[:, a2 * S:(a2 + 1) * S],
                                                                ACT.Identity, bias=col("qk"[i] + "1", a2))
                            else:
                                last = nc.scalar.activation(xb[:, i, :], bank, ACT.Copy)
                            out_of_bank(e, last)
                        elif kind == "pvv" and a > 1:
                            bank = read_bank(e)
                            out_of_bank(e, nc.scalar.activation(vaug[:, rot, :, :, 0:HD],
                                                                bank.rearrange("p (f s d) -> p f s d", f=2, s=H), ACT.Copy))
                        elif kind == "pvt":
                            bank = read_bank(e)
                            for hf in range(2):
                                dst = vaug[:, rot, i, 8 * hf:8 * hf + 8, :].rearrange("p (b h) w -> p h b w", h=2)
                                src = bank[:, hf * 256:(hf + 1) * 256].rearrange("p (h b w) -> p h b w", h=2, b=4)
                                last = nc.scalar.activation(dst, src, ACT.Copy)
                            out_of_bank(e, last)
                        elif kind == "ctr":
                            bank = read_bank(e)
                            if a == 3:
                                last = nc.scalar.activation(cT[:, rot].rearrange("p a b -> p (a b)"), bank, ACT.Copy)
                            else:
                                for dst, g, b in ((cT[:, rot], "gk", "bk"), (vT[:], "gv", "bv")):
                                    for dk in range(2):
                                        last = nc.scalar.activation(dst[:, dk, :], bank[:, dk * S:(dk + 1) * S], ACT.Identity,
                                                                    scale=col(g, dk), bias=col(b, dk))
                            out_of_bank(e, last)
                        elif kind == "st":
                            act.wait_ge(st_done, NTH[e])
                            k = NTH[e] - 1
                            if k >= PT_SLOTS:
                                act.wait_ge(pv_done, (k - PT_SLOTS) // 4 + 1)
                            nc.scalar.activation(pt[:, k % PT_SLOTS], ps_st[:, i % 2], ACT.Exp, scale=SCALE).then_inc(exp_done, 1)
                        elif kind == "pvout":
                            act.wait_ge(pv_done, NTH["pvg", n, 2 * i + 1])
                            if n > 0:
                                wait_filled(act, ("otr", n - 1, 1))
                            nc.scalar.activation(ote[:, i], ps_pv[:, i], ACT.Copy).then_inc(ote_ready, 1)
                        elif kind == "ott" and a > 0:
                            out_of_bank(e, nc.scalar.activation(ot[:].rearrange("p a b -> p (a b)"), read_bank(e), ACT.Copy))
                        elif kind == "xtr":
                            bank = read_bank(e)
                            if a == 5:
                                for dk in range(2):
                                    last = nc.scalar.activation(xT[:, u % 2, dk, :], bank[:, dk * S:(dk + 1) * S], ACT.Identity,
                                                                scale=col("gh", dk), bias=col("bh", dk))
                            else:
                                last = nc.scalar.activation(xT[:, u % 2].rearrange("p a b -> p (a b)"), bank, ACT.Copy)
                            out_of_bank(e, last)
                        elif kind == "ff1":
                            bank = read_bank(e)
                            for c in range(2):
                                last = nc.scalar.activation(hT[:, 2 * i + c, :], bank[:, c * S:(c + 1) * S],
                                                            ACT.Tanh if a == 1 else ACT.Relu, bias=col("u" + str(a), 2 * i + c))
                            out_of_bank(e, last)

                @block.vector
                def _(dve):
                    chain = [0]

                    def link(ins):
                        chain[0] += 1
                        ins.then_inc(dve_link, 1)
                        dve.wait_ge(dve_link, chain[0])

                    def read_bank(e):
                        wait_filled(dve, e)
                        return ps_misc[:, MISC[e][0], :]

                    def out_of_bank(e, last):
                        last.then_inc(misc_out[MISC[e][0]], 1)

                    def moments(src, k, eps, done):
                        for hf in range(2):
                            last = nc.vector.bn_stats(stats[:, k, hf, :], src[:, hf, :])
                        link(last)
                        for hf in range(2):
                            last = nc.vector.bn_aggr(mv[:, k, hf, :], stats[:, k, hf, :])
                        link(last)
                        nc.vector.tensor_scalar(var[:, k, :], mv[:, k, :, 1], eps, None, ALU.add).then_inc(done, 1)

                    def normalise(dst, src, k, done):
                        for hf in range(2):
                            last = nc.vector.tensor_scalar(dst[:, hf, :], src[:, hf, :], mv[:, k, hf, 0:1], rstd[:, k, hf:hf + 1],
                                                           ALU.subtract, ALU.mult)
                        last.then_inc(done, 1)

                    dve.wait_ge(pad_loaded, 16)
                    nc.vector.tensor_scalar(pen_row[0:NB, :], pad_i[:], 0.0, NEG, ALU.is_equal, ALU.mult).then_inc(pad_made, 1)
                    for e in ORDER:
                        kind, n, i = e
                        a, u, rot = n // NB, n % NB, n % 2
                        x = xn[:, u]
                        if kind == "pqk" and a == 0:
                            bank = read_bank(e)
                            if n > 0:
                                dve.wait_ge(lo_done, NTH["mid", n - 1, i])
                            dst = xb[:, i, :].rearrange("p (h c r) -> p c h r", h=2, r=16)
                            out_of_bank(e, nc.vector.transpose(dst, bank.rearrange("p (c h r) -> p c h r", h=2, r=16)))
                        elif kind == "hi":
                            if a == 0:
                                dve.wait_ge(xb_biased, NTH["pqk", n, i])
                            else:
                                wait_out(dve, ("pqk", n, i))
                            if n > 0:
                                dve.wait_ge(scr_written[(n - 1) % 2][i], 16 * written(n - 1))
                            nc.vector.tensor_copy(parts[:, i, 0, :], xb[:, i, :]).then_inc(hi_done, 1)
                        elif kind == "mid":
                            dve.wait_ge(rest_done, NTH["hi", n, i])
                            nc.vector.tensor_copy(parts[:, i, 1, :], xb[:, i, :]).then_inc(mid_done, 1)
                        elif kind == "e0":
                            wait_out(dve, ("pqk", n, 0))
                            for a2 in range(2):
                                last = nc.vector.tensor_scalar(q0blk[:, a2, :], headsel[:, a2, :], xb[:, 0, a2 * S:a2 * S + 1],
                                                               None, ALU.mult)
                            last.then_inc(q0_ready, 1)
                        elif kind == "len":
                            e0 = ("e0", n, 0)
                            bank = read_bank(e0)
                            k = FF3_BEFORE[n]
                            if k:
                                dve.wait_ge(ff3_done, k)
                            out_of_bank(e0, nc.vector.tensor_scalar(nonzero, bank[0:H, 0:S], 0.0, None, ALU.not_equal))
                            wait_out(dve, e0)
                            link(nc.vector.reduce_sum(length[:], nonzero, AX))
                            dve.wait_ge(stack_ready[rot][1], parity(n - 2, 112))
                            nc.vector.tensor_scalar(pen16[:, rot, :], iota[:], length[:, 0:1], NEG, ALU.is_ge,
                                                    ALU.mult).then_inc(pen_ready, 1)
                        elif kind == "pvv" and a <= 1:
                            bank = read_bank(e)
                            bias = tile2("v" + str(a)).rearrange("p f (s d) -> p f s d", d=HD)
                            out_of_bank(e, nc.vector.tensor_tensor(vaug[:, rot, :, :, 0:HD],
                                                                   bank.rearrange("p (f s d) -> p f s d", f=2, s=H), bias, ALU.add))
                            if a == 0:
                                wait_out(dve, e)
                                for hf in range(2):
                                    last = nc.vector.transpose(vflip[:, hf, :].rearrange("p (h c r) -> p c h r", h=2, r=16),
                                                               vaug[:, rot, hf].rearrange("p s (h r) -> p s h r", r=16))
                                last.then_inc(v_flipped, 1)
                        elif kind == "ctr" and a == 3:
                            dve.wait_ge(cn_loaded, 16 * (u + 1))
                            dve.wait_ge(msk_done, NTH["msk", n - NB, 0])
                            for hf in range(2):
                                last = nc.vector.tensor_scalar(cn[:, hf, :], cn[:, hf, :], tmask[:, u, 1, hf:hf + 1], None, ALU.mult)
                            last.then_inc(cmask_done, 1)
                        elif kind == "clnA":
                            dve.wait_ge(cn_loaded, 16 * (NB + u + 1))
                            moments(cn, NB, EPS, cln_var)
                        elif kind == "clnB":
                            dve.wait_ge(cln_rstd, u + 1)
                            normalise(cn, cn, NB, cln_hat)
                        elif kind == "nat":
                            dve.wait_ge(nat_done, NTH[e])
                            nc.vector.reduce_max(mraw[:, i // 8, :, i % 8], ps_nat[:, i % 2], AX).then_inc(max_done, 1)
                        elif kind == "neg":
                            dve.wait_ge(max_done, NTH["nat", n, 8 * i + 7])
                            nc.vector.tensor_scalar(negm[:, i, :], mraw[:, i].rearrange("p f s -> p (f s)"), FLOOR, -1.0,
                                                    ALU.max, ALU.mult).then_inc(neg_done, 1)
                        elif kind == "nmt":
                            bank = read_bank(e)
                            if n > 0:
                                dve.wait_ge(shift_ready[(n - 1) % 2][i], parity(n - 1, 32))
                            out_of_bank(e, nc.vector.tensor_copy(negm_t[:, i, :], bank[0:16, 0:P]))
                        elif kind == "otr":
                            bank = read_bank(e).rearrange("p (s w) -> p s w", w=32)
                            link(nc.vector.reciprocal(rec[:, i, :], bank[:, :, HD]))
                            if a in (2, 3):
                                dve.wait_ge(msk_done, NTH["msk", n - NB, 0])
                                link(nc.vector.tensor_scalar(rec[:, i, :], rec[:, i, :], tmask[:, u, a - 2, i:i + 1], None, ALU.mult))
                            if n >= 1 and ("res", n - 1, 0) in NTH:
                                dve.wait_ge(res_done, NTH["res", n - 1, 0])
                            src = bank[:, :, 0:HD]
                            by = rec[:, i, :].unsqueeze(2).to_broadcast([P, H, HD])
                            if a == 0:
                                dst = on0[:, i, :, 0:HD]
                            elif a in (2, 3):
                                dst = on[:, i, :].rearrange("p (a h d) -> p h a d", a=2, d=HD)
                                src = src.rearrange("p (h a) d -> p h a d", a=2)
                                by = rec[:, i, :].rearrange("p (h a) -> p h a", a=2).unsqueeze(3).to_broadcast([P, H // 2, 2, HD])
                            else:
                                dst = on[:, i, :].rearrange("p (s d) -> p s d", d=HD)
                            out_of_bank(e, nc.vector.tensor_tensor(dst, src, by, ALU.mult))
                        elif kind == "ott" and a == 0:
                            wait_out(dve, ("otr", n, 0))
                            wait_out(dve, ("otr", n, 1))
                            if n + 1 < NB:
                                wait_filled(dve, ("pvt", n + 1, 1))
                            for hf in range(2):
                                last = nc.vector.transpose(ot0[:, hf, :].rearrange("p (c s r) -> p s c r", c=2, r=16),
                                                           on0[:, hf].rearrange("p s (c r) -> p s c r", r=16))
                            last.then_inc(ot0_ready, 1)
                        elif kind == "opr":
                            bank = read_bank(e)
                            if a <= 1:
                                dve.wait_ge(bias_done, NTH["pb", n, 0])
                            else:
                                dve.wait_ge(ln_done, LN_DONE[n - NB, 2 if a == 4 else 0])
                            out_of_bank(e, nc.vector.tensor_tensor(x, bank.rearrange("p (f d) -> p f d", f=2), x, ALU.add))
                        elif kind == "lnA":
                            if a in (2, 3) and i == 0:
                                dve.wait_ge(res_done, NTH["res", n, 0])
                            elif a == 1 and i == 1:
                                wait_out(dve, ("ff2", n, 0))
                                wait_out(dve, ("ff2", n, 1))
                            elif a == 3 and i == 1:
                                dve.wait_ge(ff3_done, 2 * (u + 1))
                            elif a == 3 and i == 2:
                                dve.wait_ge(ln_done, LN_DONE[n, 1])
                            else:
                                wait_out(dve, ("opr", n, 0))
                            moments(x, u, 0.0 if a == 0 else EPS, ln_var)
                        elif kind == "lnB":
                            dve.wait_ge(ln_rstd, NTH["lnA", n, i])
                            if a == 0:
                                link(nc.vector.tensor_scalar(rstd[:, u, :], rstd[:, u, :], 1e-8, None, ALU.add))
                                link(nc.vector.reciprocal(rstd[:, u, :], rstd[:, u, :]))
                            if a == 5:
                                wait_filled(dve, ("xtr", n - 1, 0) if u else ("ctr", NU - 1, 0))
                            normalise(hbuf if a == 5 else x, x, u, ln_hat)
                        elif kind == "ff2":
                            bank = read_bank(e)[:, 0:D]
                            if a == 3:
                                if u or i:
                                    dve.wait_ge(ff3_done, 2 * u + i)
                                out_of_bank(e, nc.vector.tensor_tensor(zt[:], bank, tile("d3"), ALU.add))
                                wait_out(dve, e)
                                dve.wait_ge(ln_done, LN_DONE[n, 0])
                                nc.vector.scalar_tensor_tensor(x[:, i, :], zt[:], tmask[:, u, 0, i:i + 1], x[:, i, :],
                                                               op0=ALU.mult, op1=ALU.add).then_inc(ff3_done, 1)
                            else:
                                dve.wait_ge(bias_done, NTH["pb", n, 1 if a == 1 else 0])
                                out_of_bank(e, nc.vector.tensor_tensor(x[:, i, :], bank, x[:, i, :], ALU.add))
                        elif kind == "msk":
                            dve.wait_ge(ln_done, LN_DONE[n, 1 if a == 1 else 0])
                            m = tmask[:, u, a - 1, :]
                            link(nc.vector.tensor_reduce(m, x, AX, ALU.max, apply_absolute_value=True))
                            nc.vector.tensor_scalar(m, m, 0.0, None, ALU.not_equal).then_inc(msk_done, 1)

                @block.gpsimd
                def _(pool):
                    chain = [0]

                    def link(ins):
                        chain[0] += 1
                        ins.then_inc(pool_link, 1)
                        pool.wait_ge(pool_link, chain[0])

                    for e in ORDER:
                        kind, n, i = e
                        a, u, rot = n // NB, n % NB, n % 2
                        x = xn[:, u]
                        if kind == "pqk" and a == 0:
                            wait_out(pool, e)
                            v = xb[:, i, :].rearrange("p (h c r) -> p h c r", h=2, r=16)
                            bias = cols[:, COFF["qk0"]:COFF["qk0"] + 16].unsqueeze(1).unsqueeze(3).to_broadcast([P, 2, 16, 16])
                            nc.gpsimd.tensor_tensor(v, v, bias, ALU.add).then_inc(xb_biased, 1)
                        elif kind == "hi":
                            pool.wait_ge(hi_done, NTH[e])
                            if a in (2, 3):
                                wait_filled(pool, ("e0", n, 0))
                            nc.gpsimd.tensor_tensor(xb[:, i, :], xb[:, i, :], parts[:, i, 0, :], ALU.subtract).then_inc(rest_done, 1)
                        elif kind == "mid":
                            pool.wait_ge(mid_done, NTH[e])
                            nc.gpsimd.tensor_tensor(parts[:, i, 2, :], xb[:, i, :], parts[:, i, 1, :], ALU.subtract).then_inc(lo_done, 1)
                        elif kind == "pb":
                            if a == 0:
                                pool.wait_ge(x_loaded[u], 16)
                                bias = tile2("o0")
                            elif a == 1 and i == 0:
                                wait_filled(pool, ("xtr", n - NB, 0))
                                bias = tile2("o1")
                            elif a == 1:
                                wait_filled(pool, ("xtr", n, 0))
                                bias = tile2("d1")
                            else:
                                pool.wait_ge(ln_hat, NTH["lnB", n, 0])
                                bias = tile2("d5")
                            nc.gpsimd.tensor_tensor(x, x, bias, ALU.add).then_inc(bias_done, 1)
                        elif kind == "res":
                            wait_out(pool, ("otr", n, 0))
                            wait_out(pool, ("otr", n, 1))
                            pool.wait_ge(ln_done, LN_DONE[n - NB, 1 if a == 2 else 0])
                            nc.gpsimd.tensor_tensor(x, x, on[:], ALU.add).then_inc(res_done, 1)
                        elif kind == "lnA":
                            pool.wait_ge(ln_var, NTH[e])
                            nc.gpsimd.tensor_tensor(rstd[:, u, :], var[:, u, :], half_pow[:, 1 if a == 0 else 0, :],
                                                    ALU.pow).then_inc(ln_rstd, 1)
                        elif kind == "clnA":
                            pool.wait_ge(cln_var, NTH[e])
                            nc.gpsimd.tensor_tensor(rstd[:, NB, :], var[:, NB, :], half_pow[:, 0, :], ALU.pow).then_inc(cln_rstd, 1)
                        elif kind == "lnB" and a < 5:
                            pool.wait_ge(ln_hat, NTH[e])
                            k = {0: "0", 4: "40"}.get(a, str(a) + str(i))
                            if a == 2:
                                k = "20"
                            link(nc.gpsimd.tensor_tensor(x, x, tile2("g" + k), ALU.mult))
                            nc.gpsimd.tensor_tensor(x, x, tile2("b" + k), ALU.add).then_inc(ln_done, 1)

            nc.all_engine_barrier(sems_to_clear=group_sems)



def _feat(wt, cols):
    k = wt.shape[0] // P
    return np.ascontiguousarray(wt[:, cols].reshape(k, P, -1).transpose(1, 0, 2)).reshape(P, -1)


def kernel(**inputs):
    import concourse.bacc as bacc
    from concourse.bass_utils import run_bass_kernel_spmd

    v = {k: np.asarray(a) for k, a in inputs.items()}
    plain = np.arange(D)
    by_a2_d_h8 = np.array([(a2 * 8 + h8) * HD + d for a2 in range(2) for d in range(HD) for h8 in range(8)])
    by_slot = np.array([(a2 * 8 + h8) * HD + d for h8 in range(8) for a2 in range(2) for d in range(HD)])
    positions = np.array([r * 16 + c for c in range(16) for r in range(16)])

    def vec(a, n):
        return a.reshape(n, P).T

    l1, l2, l3 = "L1_xattn_", "L2_xattn_", "L3_xattn_"
    wo0 = np.zeros((P, 4, D), np.float32)
    wo0_t = v["L0_xattn_Wo"].T
    for half in range(2):
        for c2 in range(2):
            for cp in range(4):
                c = half * 8 + cp * 2 + c2
                wo0[32 * cp:32 * cp + HD, half * 2 + c2] = wo0_t[c * HD:(c + 1) * HD]

    def heads(name):
        return v[l2 + name].transpose(1, 0, 2).reshape(D, D)

    inw, inb = v[l1 + "in_proj_w"], v[l1 + "in_proj_b"]
    w = {"q0": _feat(v["L0_xattn_Wq"].T, plain), "k0": _feat(v["L0_xattn_Wk"].T, plain),
         "v0": _feat(v["L0_xattn_Wv"].T, plain), "o0": wo0.reshape(P, -1),
         "q1": _feat(inw[:D].T, by_a2_d_h8), "k1": _feat(inw[D:2 * D].T, by_a2_d_h8), "v1": _feat(inw[2 * D:].T, by_slot),
         "o1": _feat(v[l1 + "out_proj_w"].T[by_slot], plain),
         "u1": _feat(v[l1 + "w1"].T, np.arange(DF)), "d1": _feat(v[l1 + "w2"].T, plain),
         "u3": _feat(v[l2 + "fc1_w"].T, plain), "d3": _feat(v[l2 + "fc2_w"].T, plain),
         "u5": _feat(v[l3 + "ffn_w1"].T, np.arange(DF)), "d5": _feat(v[l3 + "ffn_w2"].T, plain)}
    for a, k in ((2, "1"), (3, "2")):
        w[f"q{a}"], w[f"k{a}"] = _feat(heads("Wq" + k), by_a2_d_h8), _feat(heads("Wk" + k), by_a2_d_h8)
        w[f"v{a}"] = _feat(heads("Wv" + k), by_slot)
    for a, k in ((4, "sa_"), (5, "ca_")):
        w[f"q{a}"], w[f"k{a}"] = _feat(v[l3 + k + "wq"].T, by_a2_d_h8), _feat(v[l3 + k + "wk"].T, by_a2_d_h8)
        w[f"v{a}"] = _feat(v[l3 + k + "wv"].T, by_slot)
        w[f"o{a}"] = _feat(v[l3 + k + "wo"].T[by_slot], plain)
    tiles = {"v0": v["L0_xattn_bv"], "o0": v["L0_xattn_bo"], "g0": v["L0_xattn_gamma"], "b0": v["L0_xattn_beta"],
             "v1": inb[2 * D:][by_slot], "o1": v[l1 + "out_proj_b"], "g10": v[l1 + "ln1_w"], "b10": v[l1 + "ln1_b"],
             "d1": v[l1 + "b2"], "g11": v[l1 + "ln2_w"], "b11": v[l1 + "ln2_b"],
             "g20": v[l2 + "ln1_g"], "b20": v[l2 + "ln1_b"], "g30": v[l2 + "ln2_g"], "b30": v[l2 + "ln2_b"],
             "g31": v[l2 + "ln3_g"], "b31": v[l2 + "ln3_b"], "d3": v[l2 + "fc2_b"],
             "g32": v[l3 + "g_sa"], "b32": v[l3 + "b_sa"], "g40": v[l3 + "g_qca"], "b40": v[l3 + "b_qca"],
             "d5": v[l3 + "ffn_b2"]}
    bq, bk = v["L0_xattn_bq"].reshape(16, HD).T, v["L0_xattn_bk"].reshape(16, HD).T
    cols = {"qk0": np.tile(np.concatenate([bq, bk]), (4, 1)),
            "q1": vec(inb[:D][by_a2_d_h8], 2), "k1": vec(inb[D:2 * D][by_a2_d_h8], 2),
            "u1": vec(v[l1 + "b1"], 8), "u3": vec(v[l2 + "fc1_b"], 2), "u5": vec(v[l3 + "ffn_b1"], 8),
            "gk": vec(v[l3 + "g_kca"], 2), "bk": vec(v[l3 + "b_kca"], 2), "gv": vec(v[l3 + "g_vca"], 2),
            "bv": vec(v[l3 + "b_vca"], 2), "gh": vec(v[l3 + "g_out"], 2), "bh": vec(v[l3 + "b_out"], 2)}

    def tokens(a):
        return a.reshape(ITERS, NB, 2, P, D).transpose(0, 1, 3, 2, 4)

    def features(a):
        return a.reshape(ITERS, NB, S, 2, P).transpose(0, 1, 4, 3, 2)

    attn = v["mask_1x1xSxS2_ik0"][0, 0][positions][:, positions]
    halves = lambda m: m.reshape(2, P, S).transpose(1, 0, 2).reshape(P, 2 * S)
    later = (np.arange(S)[None, :] > np.arange(S)[:, None]).astype(np.float32)
    headsel = np.zeros((P, 2, H), np.float32)
    for p in range(P):
        for a2 in range(2):
            headsel[p, a2, (p % 8) * 2 + a2] = 1
    arrays = {
        "x": tokens(v["x"]), "x_t": features(v["x"]), "ctx": tokens(v["ctx_1024"]), "ctx_t": features(v["ctx_1024"]),
        "attn": np.stack([halves(attn), halves(attn.T)], 1),
        "causal": np.stack([halves(later), halves(later.T)], 1),
        "pad": v["mask_Bx1x1xS2_ik0"][:, 0, 0][:, positions].reshape(ITERS, NB, S),
        "weights": np.concatenate([w[k] for k, _ in WEIGHTS], 1),
        "tiles": np.stack([tiles[k] for k in TILES]),
        "cols": np.concatenate([cols[k] for k, _ in COLS], 1),
        "ident": np.eye(P, dtype=np.float32), "headsel": headsel,
        "iota": np.tile(np.arange(S, dtype=np.float32), (H, 1)),
        "half_pow": np.tile(np.array([[-0.5, -0.5], [0.5, 0.5]], np.float32), (P, 1, 1)),
    }
    arrays = {k: np.ascontiguousarray(a) for k, a in arrays.items()}
    nc = bacc.Bacc("TRN2", target_bir_lowering=False, num_devices=1, dynamic_dma_scratch_size=1024)
    t = {k: nc.dram_tensor("in_" + k, a.shape, mybir.dt.from_np(a.dtype), kind="ExternalInput").ap() for k, a in arrays.items()}
    t["out"] = nc.dram_tensor("out", (ITERS, NB, P, 2, D), F32, kind="ExternalOutput").ap()
    t["scratch"] = nc.dram_tensor("scratch", (2, 2, 3, HD, H, S), BF16, kind="Internal").ap()
    block_kernel(nc, t)
    r = run_bass_kernel_spmd(nc, [{"in_" + k: a for k, a in arrays.items()}], core_ids=[0])
    out = r.results[0]["out"]
    return np.ascontiguousarray(out.transpose(0, 1, 3, 2, 4)).reshape(B, S, D)
```

```python
from contextlib import ExitStack

import numpy as np

import concourse.bass as bass
from concourse import mybir

P = 128
B, S, D, H = 16, 256, 256, 16
HD = D // H
DF = 4 * D
NB = 4
ITERS = B // NB
NA = 6
NU = NA * NB
SCALE = float(HD) ** -0.5
NEG = -1.0e30
FLOOR = -1.0e28
EPS = 1e-5
ROWS = 6 * HD
PEN, SHIFT = ROWS, ROWS + 1
PT_SLOTS = 6
LO, HI, MID = range(3)
LAG = 13
AHEAD = 18
NMT_AT = 9
PVG_AT = 5
CUT = 72
NO_PEN = 32

F32 = mybir.dt.float32
BF16 = mybir.dt.bfloat16
I32 = mybir.dt.int32
ALU = mybir.AluOpType
ACT = mybir.ActivationFunctionType
AX = mybir.AxisListType.X

WEIGHTS = [("q0", 512), ("k0", 512), ("v0", 512), ("o0", 1024),
           ("q1", 512), ("k1", 512), ("v1", 512), ("o1", 512), ("u1", 2048), ("d1", 2048),
           ("q2", 512), ("k2", 512), ("v2", 512), ("q3", 512), ("k3", 512), ("v3", 512), ("u3", 512), ("d3", 512),
           ("q4", 512), ("k4", 512), ("v4", 512), ("o4", 512), ("q5", 512), ("k5", 512), ("v5", 512), ("o5", 512),
           ("u5", 2048), ("d5", 2048)]
WOFF, WCOLS = {}, 0
for _name, _n in WEIGHTS:
    WOFF[_name] = WCOLS
    WCOLS += _n
W_PARTS = [(0, WOFF["q1"]), (WOFF["q1"], WOFF["q2"]), (WOFF["q2"], WCOLS)]
PIECE = 1024
PIECES = [(_k, _lo, min(_lo + PIECE, _hi)) for _k in (1, 2) for _lo in range(W_PARTS[_k][0], W_PARTS[_k][1], PIECE)
          for _hi in (W_PARTS[_k][1],)]
TILES = ["v0", "o0", "g0", "b0", "v1", "o1", "g10", "b10", "d1", "g11", "b11", "g20", "b20", "g30", "b30",
         "g31", "b31", "d3", "g32", "b32", "g40", "b40", "d5"]
COLS = [("qk0", 16), ("q1", 2), ("k1", 2), ("u1", 8), ("u3", 2), ("u5", 8),
        ("gk", 2), ("bk", 2), ("gv", 2), ("bv", 2), ("gh", 2), ("bh", 2)]
COFF, NCOLS = {}, 0
for _name, _n in COLS:
    COFF[_name] = NCOLS
    NCOLS += _n

POST = {
    0: [("ldx", 0, -8.5), ("otr", 0, -2), ("pb", 0, -0.5), ("otr", 1, 2.5), ("ott", 0, 5.5), ("opr", 0, 6.5),
        ("lnA", 0, 7.75), ("lnB", 0, 8), ("xtr", 0, 12)],
    1: [("otr", 0, -2), ("pb", 0, 0), ("otr", 1, 3), ("ott", 0, 3.5), ("opr", 0, 5), ("lnA", 0, 6.25), ("lnB", 0, 7),
        ("xtr", 0, 11), ("pb", 1, 12), ("ff1", 0, 13), ("ff1", 1, 13), ("ff1", 2, 14), ("ff1", 3, 14), ("ff2", 0, 16),
        ("ff2", 1, 17), ("lnA", 1, 17.25), ("lnB", 1, 18), ("xtr", 1, 21), ("msk", 0, 22)],
    2: [("otr", 0, -2), ("otr", 1, 3), ("res", 0, 5), ("lnA", 0, 6.25), ("lnB", 0, 7), ("xtr", 0, 11), ("msk", 0, 14)],
    3: [("otr", 0, -2), ("otr", 1, 3.5), ("res", 0, 4.5), ("lnA", 0, 5.75), ("lnB", 0, 6.5), ("xtr", 0, 10),
        ("ff1", 0, 12.75), ("ff2", 0, 14.5), ("ff2", 1, 15.5), ("lnA", 1, 15.75), ("lnB", 1, 16.5), ("lnA", 2, 18.75),
        ("lnB", 2, 19.5), ("xtr", 1, 22.5)],
    4: [("otr", 0, -2), ("otr", 1, 2), ("ott", 0, 3.5), ("opr", 0, 5), ("lnA", 0, 6.25), ("lnB", 0, 7),
        ("xtr", 0, 12)],
    5: [("otr", 0, -2.75), ("otr", 1, 1.75), ("ott", 0, 3.75), ("opr", 0, 4.75), ("lnA", 0, 5.75), ("lnB", 0, 6.75),
        ("pb", 0, 7.75), ("xtr", 0, 8.75), ("ff1", 0, 9.75), ("ff1", 1, 11.25), ("ff1", 2, 13.25), ("ff1", 3, 13.25),
        ("ff2", 0, 16.25), ("ff2", 1, 17.25), ("store", 0, 17.75)],
}


PRE = {
    0: [("pad", 0, 0), ("load", 0, 0), ("pqk", 0, 7), ("pqk", 1, 8), ("hi", 0, 8.5), ("hi", 1, 8.5), ("swr", 0, 8.5),
        ("mid", 0, 10.25), ("mid", 1, 10.75), ("swr", 1, 11.25), ("srd", 0, 12.25), ("srd", 1, 16.25),
        ("pvv", 0, 17.25), ("pvt", 0, 20), ("pvt", 1, 20.25)],
    1: [("load", 0, 0), ("pqk", 0, 7), ("pqk", 1, 8), ("hi", 0, 9), ("hi", 1, 9), ("mid", 0, 10.75), ("swr", 0, 10.75),
        ("mid", 1, 11.25), ("swr", 1, 11.75), ("srd", 0, 12.75), ("srd", 1, 16.75), ("pvv", 0, 17.75)],
    2: [("pqk", 0, 7), ("pqk", 1, 7.75), ("e0", 0, 8.5), ("hi", 0, 9), ("hi", 1, 9), ("mid", 0, 9.75), ("len", 0, 10),
        ("swr", 0, 10.75), ("mid", 1, 11.25), ("swr", 1, 11.75), ("srd", 0, 12.75), ("srd", 1, 16.5),
        ("pvv", 0, 17.5)],
    3: [("load", 0, 0), ("ctr", 0, 4.5), ("pqk", 0, 7), ("pqk", 1, 7.75), ("e0", 0, 8.5), ("hi", 0, 9), ("hi", 1, 9),
        ("len", 0, 10), ("mid", 0, 10.75), ("swr", 0, 10.75), ("mid", 1, 11.25), ("swr", 1, 11.75), ("srd", 0, 12.25),
        ("srd", 1, 16.25), ("pvv", 0, 17.25)],
    4: [("pqk", 0, 6.75), ("pqk", 1, 8), ("hi", 0, 9), ("hi", 1, 9), ("swr", 0, 10), ("mid", 0, 10.75),
        ("mid", 1, 11.25), ("swr", 1, 11.75), ("srd", 0, 12.75), ("srd", 1, 16.75), ("pvv", 0, 18.25)],
    5: [("load", 0, 0), ("clnA", 0, 1), ("clnB", 0, 2), ("ctr", 0, 3.5), ("pqk", 0, 7), ("pqk", 1, 8), ("hi", 0, 8.5),
        ("hi", 1, 8.5), ("mid", 0, 10.25), ("swr", 0, 10.25), ("mid", 1, 10.75), ("swr", 1, 11.25), ("srd", 0, 12.25),
        ("srd", 1, 16.25), ("pvv", 0, 17.75)],
}


FIRST = {"nmt": 0, "nat": 4, "neg": 4, "st": 5, "pvg": 6, "pvout": 7}


def plan():
    out = []

    def add(at, kind, n, i, order=None):
        out.append((at, FIRST.get(kind, order), len(out), (kind, n, i)))

    for n in range(NU):
        for kind, i, at in POST[n // NB]:
            add((n + 1) * 16 + LAG + at, kind, n, i, 1)
        for kind, i, at in PRE[n // NB]:
            if kind != "pad" or n == 0:
                add(n * 16 - AHEAD + at, kind, n, i, 2)
        for s in range(16):
            add(n * 16 + s, "nat", n, s)
            add(n * 16 + LAG + s, "st", n, s)
        for half in range(2):
            add(n * 16 + 8 * half + 7, "neg", n, half)
            add(n * 16 + 8 * half + NMT_AT, "nmt", n, half)
            add(n * 16 + LAG + 8 * half + 4 + PVG_AT, "pvout", n, half)
        for g in range(4):
            add(n * 16 + LAG + 4 * g + PVG_AT, "pvg", n, g)
    return out


def attention(n):
    return n % NU // NB


def own_penalty(n):
    a = attention(n)
    return a in (0, 2, 3) or a in (1, 4) and n % NB < 2


MISC_KINDS = ("nmt", "pqk", "pvv", "pvt", "ctr", "e0", "otr", "ott", "opr", "xtr", "ff1", "ff2")


class Window:

    def __init__(self, stages):
        self.order = [e for *_, e in sorted(stages)]
        self.place = {e: k for k, e in enumerate(self.order)}
        self.kinds, self.bank = {}, {}
        for e in self.order:
            self.kinds.setdefault(e[0], []).append(e)
            if e[0] in MISC_KINDS and not (e[0] == "ott" and attention(e[1]) == 0):
                k = len(self.bank)
                self.bank[e] = k % 2, k // 2 + 1
        assert all(("len", n, 0) in self.place for kind, n, _ in self.order if kind == "e0")

    def nth(self, e, like=lambda n, i: True):
        if e not in self.place:
            return 0
        return sum(like(n, i) for kind, n, i in self.kinds[e[0]] if self.place[kind, n, i] <= self.place[e])

    def before(self, e, kind, like):
        return sum(like(n, i) for _, n, i in self.kinds.get(kind, ()) if self.place[kind, n, i] < self.place[e])

    def total(self, kind, like, each=lambda n: 1):
        return sum(each(n) for _, n, i in self.kinds.get(kind, ()) if like(n, i))


_plan = plan()
_next = [(at + 16 * NU, order, k, (kind, n + NU, i)) for at, order, k, (kind, n, i) in _plan]
PIECES[6:6] = [("tiles", _lo, min(_lo + 5, len(TILES))) for _lo in range(4, len(TILES), 5)]
_pieces = [(-4 + 2.5 * k, 9, k, ("wld", 0, k)) for k in range(len(PIECES))]
HEAD = Window([p for p in _plan if p[0] < CUT] + _pieces)
BODY = Window([p for p in _plan + _next if CUT <= p[0] < CUT + 16 * NU])
TAIL = Window([p for p in _plan if p[0] >= CUT])
assert len(HEAD.order) - len(PIECES) + len(TAIL.order) == len(BODY.order) == len(_plan)


def block_kernel(nc, t):
    with ExitStack() as ctx:
        def sb(name, shape, dt=F32):
            return ctx.enter_context(nc.sbuf_tensor(name, shape, dt))

        sems = []

        def sem(name):
            s = ctx.enter_context(nc.semaphore(name))
            sems.append(s)
            return s

        weights = sb("weights", [P, WCOLS])
        tiles = sb("tiles", [P, len(TILES), D])
        cols = sb("cols", [P, NCOLS])
        ident = sb("ident", [P, P])
        ident_b = sb("ident_b", [P, P], BF16)
        mask0 = sb("mask0", [P, 2, S], BF16)
        mask0_t = sb("mask0_t", [P, 2, S], BF16)
        causal = sb("causal", [P, S], BF16)
        causal_t = sb("causal_t", [P, P], BF16)
        headsel = sb("headsel", [P, 2, H])
        iota = sb("iota", [H, S])
        half_pow = sb("half_pow", [P, 2, 2])
        xn = sb("xn", [P, NB, 2, D])
        xT = sb("xT", [P, 2, 2, S])
        cT = sb("cT", [P, 2, 2, S])
        vT = sb("vT", [P, 2, S])
        cn = sb("cn", [P, 2, D])
        tmask = sb("tmask", [P, NB, 2, 2])
        pad_i = sb("pad_i", [NB, S], I32)
        pen_row = sb("pen_row", [NO_PEN + 1, S], BF16)
        xb = sb("xb", [P, 2, 512])
        parts = sb("parts", [P, 2, 3, 512], BF16)
        qst = sb("qst", [P, 2, H, S], BF16)
        kst = sb("kst", [P, 2, H, S], BF16)
        vaug = sb("vaug", [P, 2, 2, H, 32])
        vflip = sb("vflip", [P, 2, 512])
        q0blk = sb("q0blk", [P, 2, H])
        length = sb("length", [H, 1])
        pen16 = sb("pen16", [H, 2, S], BF16)
        mraw = sb("mraw", [P, 2, 2, 8])
        negm = sb("negm", [P, 2, 16])
        negm_t = sb("negm_t", [16, 2, P], BF16)
        pt = sb("pt", [P, PT_SLOTS, 2, S])
        ote = sb("ote", [P, 2, 2, S])
        rec = sb("rec", [P, 2, 2, H // 2])
        on = sb("on", [P, 2, D])
        on0 = sb("on0", [P, 2, H, 32])
        ot = sb("ot", [P, 2, S])
        stats = sb("stats", [P, NB + 1, 2, 6])
        mv = sb("mv", [P, NB + 1, 2, 2])
        var = sb("var", [P, NB + 1, 2])
        rstd = sb("rstd", [P, NB + 1, 2])
        hbuf = cn
        hT = sb("hT", [P, 8, S])
        ot0 = hT[:, 0:4, :].rearrange("p (f k) s -> p f (k s)", f=2)
        zt = sb("zt", [P, D])
        nonzero = zt[0:H, :]

        ps_nat = ctx.enter_context(nc.psum_tensor("ps_nat", [P, 2, 2, S], F32))
        ps_st = ctx.enter_context(nc.psum_tensor("ps_st", [P, 2, 2, S], F32))
        ps_pv = ctx.enter_context(nc.psum_tensor("ps_pv", [P, 2, 2, S], F32))
        ps_misc = ctx.enter_context(nc.psum_tensor("ps_misc", [P, 2, 512], F32))

        w_loaded = [ctx.enter_context(nc.semaphore(f"w_loaded{i}")) for i in range(len(W_PARTS))]
        const_loaded = ctx.enter_context(nc.semaphore("const_loaded"))
        const_made = ctx.enter_context(nc.semaphore("const_made"))
        fill_done = ctx.enter_context(nc.semaphore("fill_done"))
        tiles_loaded = ctx.enter_context(nc.semaphore("tiles_loaded"))
        raw_masks = ctx.enter_context(nc.semaphore("raw_masks"))

        pad_loaded, pad_made = sem("pad_loaded"), sem("pad_made")
        x_loaded = [sem(f"x_loaded{u}") for u in range(NB)]
        xT_loaded = [sem(f"xT_loaded{r}") for r in range(2)]
        cT_loaded = [sem(f"cT_loaded{r}") for r in range(2)]
        cn_loaded, cmask_done = sem("cn_loaded"), sem("cmask_done")
        cln_var, cln_rstd, cln_hat = sem("cln_var"), sem("cln_rstd"), sem("cln_hat")
        misc_ready = [sem(f"misc_ready{b}") for b in range(2)]
        misc_out = [sem(f"misc_out{b}") for b in range(2)]
        xb_biased = sem("xb_biased")
        hi_done, rest_done, mid_done, lo_done = sem("hi_done"), sem("rest_done"), sem("mid_done"), sem("lo_done")
        q0_ready, pen_ready = sem("q0_ready"), sem("pen_ready")
        scr_written = [[sem(f"scr_written{r}{c}") for c in range(2)] for r in range(2)]
        stack_ready = [[sem(f"stack_ready{r}{h}") for h in range(2)] for r in range(2)]
        shift_ready = [[sem(f"shift_ready{r}{h}") for h in range(2)] for r in range(2)]
        v_flipped = sem("v_flipped")
        nat_done, max_done, neg_done = sem("nat_done"), sem("max_done"), sem("neg_done")
        st_done, exp_done, pv_done, ote_ready = sem("st_done"), sem("exp_done"), sem("pv_done"), sem("ote_ready")
        ot0_ready = sem("ot0_ready")
        res_done, bias_done = sem("res_done"), sem("bias_done")
        ln_var, ln_rstd, ln_hat, ln_done = sem("ln_var"), sem("ln_rstd"), sem("ln_hat"), sem("ln_done")
        ff3_done, msk_done = sem("ff3_done"), sem("msk_done")
        stored = [sem(f"stored{u}") for u in range(NB)]
        dve_link, pool_link = sem("dve_link"), sem("pool_link")
        group_sems = range(min(s.num for s in sems), max(s.num for s in sems) + 1)
        assert len(group_sems) == len(sems)

        def w(name, *dims):
            n = dict(WEIGHTS)[name]
            v = weights[:, WOFF[name]:WOFF[name] + n]
            return v.rearrange("p (a b) -> p a b", b=dims[0])

        def pieces(part):
            return sum(p[0] == part for p in PIECES)

        def tile(name):
            return tiles[:, TILES.index(name), :]

        def tile2(name):
            return tiles[:, TILES.index(name), :].unsqueeze(1).to_broadcast([P, 2, D])

        def col(name, i):
            return cols[:, COFF[name] + i:COFF[name] + i + 1]

        scr = t["scratch"]

        with nc.Block() as block:
            @block.sync
            def _(sp):
                sp.dma_start(xb[:, 0, :].bitcast(I32), t["attn"][:, 0]).then_inc(raw_masks, 16)
                sp.dma_start(xb[:, 1, :].bitcast(I32), t["attn"][:, 1]).then_inc(raw_masks, 16)
                sp.dma_start(vflip[:, 0, 0:S + P], t["causal"]).then_inc(raw_masks, 16)
                for name, dst in (("ident", ident), ("cols", cols), ("headsel", headsel), ("iota", iota),
                                  ("half_pow", half_pow)):
                    sp.dma_start(dst[:], t[name]).then_inc(const_loaded, 16)
                lo, hi = W_PARTS[0]
                sp.dma_start(weights[:, lo:hi], t["weights"][:, lo:hi]).then_inc(w_loaded[0], 16)
                sp.dma_start(tiles[:, 0:4], t["tiles"][0:4].partition_broadcast(P)).then_inc(const_loaded, 16)
                sp.wait_ge(const_loaded, 96)

            @block.vector
            def _(dve):
                dve.wait_ge(raw_masks, 48)
                nc.vector.tensor_scalar(mask0[:].rearrange("p a b -> p (a b)"), xb[:, 0, :].bitcast(I32), 0.0, NEG,
                                        ALU.is_equal, ALU.mult).then_inc(const_made, 1)
                nc.vector.tensor_scalar(mask0_t[:].rearrange("p a b -> p (a b)"), xb[:, 1, :].bitcast(I32), 0.0, NEG,
                                        ALU.is_equal, ALU.mult).then_inc(const_made, 1)
                nc.vector.tensor_scalar(causal[:], vflip[:, 0, 0:S], NEG, None,
                                        ALU.mult).then_inc(const_made, 1)
                nc.vector.tensor_scalar(causal_t[:], vflip[:, 0, S:S + P], NEG, None,
                                        ALU.mult).then_inc(const_made, 1)
                dve.wait_ge(const_loaded, 96)
                nc.vector.tensor_copy(ident_b[:], ident[:]).then_inc(const_made, 1)

            @block.gpsimd
            def _(pool):
                nc.gpsimd.memset(qst[PEN:PEN + 2], 1.0).then_inc(fill_done, 1)
                pool.wait_ge(fill_done, 1)
                nc.gpsimd.memset(kst[PEN:PEN + 2], 1.0).then_inc(fill_done, 1)
                pool.wait_ge(fill_done, 2)
                nc.gpsimd.memset(vaug[:], 0.0).then_inc(fill_done, 1)
                pool.wait_ge(fill_done, 3)
                nc.gpsimd.memset(on0[:], 0.0).then_inc(fill_done, 1)
                pool.wait_ge(fill_done, 4)
                nc.gpsimd.memset(pen_row[NO_PEN:NO_PEN + 1, :], 0.0).then_inc(fill_done, 1)
                pool.wait_ge(fill_done, 5)
                nc.gpsimd.memset(vaug[:, :, :, :, HD:HD + 1].rearrange("p a b c d -> p (a b c) d"), 1.0).then_inc(fill_done, 1)
                pool.wait_ge(fill_done, 6)

        nc.all_engine_barrier()

        def run(win, group):
            nth = win.nth

            def wait_out(eng, e):
                if e in win.bank:
                    bank, k = win.bank[e]
                    eng.wait_ge(misc_out[bank], k)

            def wait_filled(eng, e):
                if e in win.bank:
                    bank, k = win.bank[e]
                    eng.wait_ge(misc_ready[bank], k)

            def loads(n, *attentions):
                return 16 * nth(("load", n, 0), lambda m, i: m % 2 == n % 2 and attention(m) in attentions)

            def written(n, c):
                like = lambda att: lambda m, i: i == c and m % 2 == n % 2 and (attention(m) == 0) == att
                return 16 * (8 * nth(("swr", n, c), like(True)) + nth(("swr", n, c), like(False)))

            def stacked(n, half):
                like = lambda pen: lambda m, i: i == half and m % 2 == n % 2 and own_penalty(m) == pen
                return 16 * (6 * nth(("srd", n, half), like(True)) + 5 * nth(("srd", n, half), like(False)))

            def shifted(n, half):
                return 16 * nth(("nmt", n, half), lambda m, i: i == half and m % 2 == n % 2)

            def scaled(n, i):
                return nth(("lnB", n, i), lambda m, j: attention(m) < 5)

            with nc.Block() as block:

                @block.sync
                def _(sp):
                    for e in win.order:
                        kind, n, i = e
                        a, u, rot = attention(n), n % NB, n % 2
                        g = group if n < NU else group + 1
                        if kind == "pad":
                            sp.dma_start(pad_i[:], t["pad"][g]).then_inc(pad_loaded, 16)
                        elif kind == "wld":
                            part, lo, hi = PIECES[i]
                            if part == "tiles":
                                sp.dma_start(tiles[:, lo:hi], t["tiles"][lo:hi].partition_broadcast(P)).then_inc(tiles_loaded, 16)
                            else:
                                sp.dma_start(weights[:, lo:hi], t["weights"][:, lo:hi]).then_inc(w_loaded[part], 16)
                        elif kind == "load":
                            if a <= 1:
                                wait_filled(sp, ("pvv", n - 2, 0))
                                sp.dma_start(cT[:, rot], t["ctx_t"][g, u]).then_inc(cT_loaded[rot], 16)
                            if a == 0:
                                wait_filled(sp, ("pqk", n - 2, 1))
                                wait_filled(sp, ("ff1", n - NB, 3))
                                sp.dma_start(xT[:, rot], t["x_t"][g, u]).then_inc(xT_loaded[rot], 16)
                            if a in (3, 5):
                                wait_filled(sp, ("ctr", n - 1 if u else n - 1 - NB, 0))
                                sp.dma_start(cn[:], t["ctx"][g, u]).then_inc(cn_loaded, 16)
                        elif kind == "ldx":
                            if count := 16 * nth(("store", n - NB, 0), lambda m, i: m % NB == u):
                                sp.wait_ge(stored[u], count)
                            sp.dma_start(xn[:, u], t["x"][g, u]).then_inc(x_loaded[u], 16)
                        elif kind == "swr":
                            if count := nth(("mid", n, i)):
                                sp.wait_ge(lo_done, count)
                            for half in range(2):
                                if count := stacked(n - 2, half):
                                    sp.wait_ge(stack_ready[rot][half], count)
                            if a == 0:
                                for pb in range(4):
                                    for qk in range(2):
                                        r = 32 * pb + 16 * qk
                                        s0 = i * 8 + pb * 2
                                        sp.dma_start(scr[rot, qk, :, :, s0:s0 + 2, :].rearrange("i d s t -> d i (s t)"),
                                                     parts[r:r + 16, i]).then_inc(scr_written[rot][i], 16)
                            else:
                                sp.dma_start(scr[rot, i].rearrange("i d (h a) t -> (d h) i (a t)", a=2),
                                             parts[:, i]).then_inc(scr_written[rot][i], 16)
                        elif kind == "srd":
                            if count := nth(("st", n - 2, 8 * i + 7)):
                                sp.wait_ge(st_done, count)
                            for c in range(2):
                                if count := written(n, c):
                                    sp.wait_ge(scr_written[rot][c], count)
                            sl = slice(8 * i, 8 * i + 8)
                            for dst, qk, row, copies, p0, p1 in ((qst, 0, 0, 2, HI, MID), (qst, 0, 64, 1, LO, HI),
                                                                 (kst, 1, 0, 2, MID, MID), (kst, 1, 32, 3, HI, HI),
                                                                 (kst, 1, 80, 1, LO, LO)):
                                src = scr[rot, qk, p0:p1 + 1, :, sl, :].rearrange("i d s t -> (i d) (s t)")
                                rows = copies * HD * (p1 + 1 - p0)
                                if copies > 1:
                                    src = src.partition_broadcast(copies)
                                sp.dma_start(dst[row:row + rows, rot, sl, :], src).then_inc(stack_ready[rot][i], 16)
                            if own_penalty(n):
                                if a in (2, 3):
                                    if count := nth(("len", n, 0)):
                                        sp.wait_ge(pen_ready, count)
                                    src = pen16[8 * i:8 * i + 8, rot, :]
                                else:
                                    if a == 0:
                                        if count := nth(("pad", n - u, 0)):
                                            sp.wait_ge(pad_made, count)
                                    k = u if a == 0 else NO_PEN
                                    src = pen_row[k:k + 1, :].unsqueeze(1).to_broadcast([1, 8, S])
                                sp.dma_start(kst[PEN:PEN + 1, rot, sl, :], src).then_inc(stack_ready[rot][i], 16)
                        elif kind == "nmt":
                            wait_out(sp, e)
                            sp.dma_start(qst[SHIFT:SHIFT + 1, rot, 8 * i:8 * i + 8, :],
                                         negm_t[:, i, :]).then_inc(shift_ready[rot][i], 16)
                        elif kind == "store":
                            wait_out(sp, ("ff2", n, 0))
                            wait_out(sp, ("ff2", n, 1))
                            sp.dma_start(t["out"][g, u], xn[:, u]).then_inc(stored[u], 16)
                    total = win.total
                    for u in range(NB):
                        if count := 16 * total("store", lambda n, i: n % NB == u):
                            sp.wait_ge(stored[u], count)
                        if count := 16 * total("ldx", lambda n, i: n % NB == u):
                            sp.wait_ge(x_loaded[u], count)
                    if count := 16 * total("pad", lambda n, i: True):
                        sp.wait_ge(pad_loaded, count)
                    if count := 16 * total("load", lambda n, i: attention(n) in (3, 5)):
                        sp.wait_ge(cn_loaded, count)
                    for r in range(2):
                        if count := 16 * total("load", lambda n, i: n % 2 == r and attention(n) == 0):
                            sp.wait_ge(xT_loaded[r], count)
                        if count := 16 * total("load", lambda n, i: n % 2 == r and attention(n) <= 1):
                            sp.wait_ge(cT_loaded[r], count)
                        for h in range(2):
                            same = lambda n, i: n % 2 == r and i == h
                            if count := 16 * total("swr", same, lambda n: 1 if attention(n) else 8):
                                sp.wait_ge(scr_written[r][h], count)
                            if count := 16 * total("srd", same, lambda n: 5 + own_penalty(n)):
                                sp.wait_ge(stack_ready[r][h], count)
                            if count := 16 * total("nmt", same):
                                sp.wait_ge(shift_ready[r][h], count)

                @block.tensor
                def _(pe):
                    def open_bank(e):
                        bank, k = win.bank[e]
                        if k > 1:
                            pe.wait_ge(misc_out[bank], k - 1)
                        return ps_misc[:, bank, :]

                    def filled(e, last):
                        last.then_inc(misc_ready[win.bank[e][0]], 1)

                    def need_xT(n):
                        a = attention(n)
                        if a == 0:
                            if count := loads(n, 0):
                                pe.wait_ge(xT_loaded[n % 2], count)
                        else:
                            wait_out(pe, ("xtr", n - NB, 1 if a in (2, 4) else 0))

                    def need_cT(n):
                        if attention(n) <= 1:
                            if count := loads(n, 0, 1):
                                pe.wait_ge(cT_loaded[n % 2], count)
                        else:
                            wait_out(pe, ("ctr", n, 0))

                    pe.wait_ge(w_loaded[0], 16)
                    for e in win.order:
                        kind, n, i = e
                        a, u, rot = attention(n), n % NB, n % 2
                        src_x, src_c = xT[:, u % 2], cT[:, rot]
                        if kind == "pqk":
                            need_xT(n)
                            if a not in (2, 4):
                                need_cT(n)
                            if a == 1:
                                pe.wait_ge(w_loaded[1], 16 * pieces(1))
                            if a == 2:
                                pe.wait_ge(w_loaded[2], 16 * pieces(2))
                            bank = open_bank(e)
                            if a == 0:
                                out = bank.rearrange("p (c w) -> p c w", w=32)
                                for qk, src in enumerate((src_x, src_c)):
                                    for dk in range(2):
                                        last = nc.tensor.matmul(out[:, :, 16 * qk:16 * qk + 16],
                                                                src[:, dk, i * P:(i + 1) * P], w("qk"[qk] + "0", D)[:, dk, :],
                                                                start=dk == 0, stop=dk == 1)
                            else:
                                src = src_x if i == 0 or a in (2, 4) else src_c
                                wv = w("qk"[i] + str(a), P)
                                for a2 in range(2):
                                    for dk in range(2):
                                        last = nc.tensor.matmul(bank[:, a2 * S:(a2 + 1) * S], wv[:, 2 * dk + a2, :],
                                                                src[:, dk, :], start=dk == 0, stop=dk == 1)
                            filled(e, last)
                        elif kind == "e0":
                            if count := nth(e):
                                pe.wait_ge(q0_ready, count)
                            wait_out(pe, ("pqk", n, 1))
                            bank = open_bank(e)
                            for a2 in range(2):
                                last = nc.tensor.matmul(bank[0:H, 0:S], q0blk[:, a2, :], xb[:, 1, a2 * S:(a2 + 1) * S],
                                                        start=a2 == 0, stop=a2 == 1)
                            filled(e, last)
                        elif kind == "pvv":
                            src = src_x if a in (2, 4) else vT[:] if a == 5 else src_c
                            bank = open_bank(e)
                            wv = w("v" + str(a), D)
                            for hf in range(2):
                                for dk in range(2):
                                    last = nc.tensor.matmul(bank[:, hf * D:(hf + 1) * D], src[:, dk, hf * P:(hf + 1) * P],
                                                            wv[:, dk, :], start=dk == 0, stop=dk == 1)
                            filled(e, last)
                        elif kind == "pvt":
                            if count := nth(("pvv", n, 0), lambda m, j: attention(m) == 0):
                                pe.wait_ge(v_flipped, count)
                            bank = open_bank(e)
                            for hf in range(2):
                                v = vflip[:, hf, :].rearrange("p (h k) -> p h k", h=2)
                                for h2 in range(2):
                                    k = 2 * hf + h2
                                    last = nc.tensor.transpose(bank[:, k * P:(k + 1) * P], v[:, h2, i * P:(i + 1) * P], ident[:])
                            filled(e, last)
                        elif kind == "ctr":
                            if a == 3:
                                if count := nth(e, lambda m, j: attention(m) == 3):
                                    pe.wait_ge(cmask_done, count)
                            else:
                                if count := nth(("clnB", n, 0)):
                                    pe.wait_ge(cln_hat, count)
                            bank = open_bank(e)
                            for dk in range(2):
                                for hf in range(2):
                                    k = 2 * dk + hf
                                    last = nc.tensor.transpose(bank[:, k * P:(k + 1) * P], cn[:, hf, dk * P:(dk + 1) * P], ident[:])
                            filled(e, last)
                        elif kind == "nat":
                            if i % 8 == 0:
                                if count := stacked(n, i // 8):
                                    pe.wait_ge(stack_ready[rot][i // 8], count)
                            k = nth(e)
                            if k > 2:
                                pe.wait_ge(max_done, k - 2)
                            for hf in range(2):
                                keys = (hf + 1) * P if a == 2 else S
                                last = nc.tensor.matmul(ps_nat[:, i % 2, hf, 0:keys], qst[0:PEN + 1, rot, i, hf * P:(hf + 1) * P],
                                                        kst[0:PEN + 1, rot, i, 0:keys], start=True, stop=True)
                            last.then_inc(nat_done, 1)
                        elif kind == "nmt":
                            if count := nth(("neg", n, i)):
                                pe.wait_ge(neg_done, count)
                            bank = open_bank(e)
                            filled(e, nc.tensor.transpose(bank[0:16, 0:P], negm[:, i, :], ident[:]))
                        elif kind == "st":
                            if i % 8 == 0:
                                if count := shifted(n, i // 8):
                                    pe.wait_ge(shift_ready[rot][i // 8], count)
                            k = nth(e)
                            if k > 2:
                                pe.wait_ge(exp_done, k - 2)
                            bank = ps_st[:, i % 2].rearrange("p a b -> p (a b)")
                            for kh in range(2):
                                q0 = kh * P if a == 2 else 0
                                out = bank[:, kh * S:kh * S + S - q0]
                                last = nc.tensor.matmul(out, kst[0:SHIFT + 1, rot, i, kh * P:(kh + 1) * P],
                                                        qst[0:SHIFT + 1, rot, i, q0:S], start=True, stop=a not in (0, 2))
                                if a == 0:
                                    last = nc.tensor.matmul(out, ident_b[:], mask0_t[:, kh, :], start=False, stop=True)
                                elif a == 2:
                                    last = nc.tensor.matmul(out[:, 0:P], ident_b[:], causal_t[:], start=False, stop=True)
                            last.then_inc(st_done, 1)
                        elif kind == "pvg":
                            if count := nth(("st", n, 4 * i + 3)):
                                pe.wait_ge(exp_done, count)
                            if i == 0:
                                wait_out(pe, ("pvt", n, 1) if a == 0 else ("pvv", n, 0))
                                if a == 0:
                                    wait_out(pe, ("pvt", n, 0))
                            if i % 2 == 0:
                                if count := nth(("pvout", n - 1, i // 2)):
                                    pe.wait_ge(ote_ready, count)
                            for kh in range(2):
                                for j in range(4):
                                    s = 4 * i + j
                                    q0 = kh * P if a == 2 else 0
                                    last = nc.tensor.matmul(ps_pv[32 * j:32 * j + 32, i // 2, i % 2, q0:S], vaug[:, rot, kh, s, :],
                                                            pt[:, (n * H + s) % PT_SLOTS, kh, 0:S - q0], start=kh == 0, stop=kh == 1)
                            last.then_inc(pv_done, 1)
                        elif kind == "otr":
                            if count := nth(("pvout", n, i)):
                                pe.wait_ge(ote_ready, count)
                            bank = open_bank(e)
                            for hf in range(2):
                                for g in range(2):
                                    k = 2 * hf + g
                                    last = nc.tensor.transpose(bank[:, k * P:(k + 1) * P], ote[:, i, g, hf * P:(hf + 1) * P], ident[:])
                            filled(e, last)
                        elif kind == "ott" and a > 0:
                            wait_out(pe, ("otr", n, 0))
                            wait_out(pe, ("otr", n, 1))
                            bank = open_bank(e)
                            for ch in range(2):
                                for hf in range(2):
                                    k = 2 * ch + hf
                                    last = nc.tensor.transpose(bank[:, k * P:(k + 1) * P], on[:, hf, ch * P:(ch + 1) * P], ident[:])
                            filled(e, last)
                        elif kind == "opr":
                            if a == 0:
                                if count := nth(("ott", n, 0), lambda m, j: attention(m) == 0):
                                    pe.wait_ge(ot0_ready, count)
                            else:
                                wait_out(pe, ("ott", n, 0))
                            bank = open_bank(e)
                            wo = w("o" + str(a), D)
                            for th in range(2):
                                for k in range(4 if a == 0 else 2):
                                    if a == 0:
                                        v = ot0[:, k // 2, :].rearrange("p (c s) -> p c s", c=2)
                                        lhs = v[:, k % 2, th * P:(th + 1) * P]
                                    else:
                                        lhs = ot[:, k, th * P:(th + 1) * P]
                                    last = nc.tensor.matmul(bank[:, th * D:(th + 1) * D], lhs, wo[:, k, :],
                                                            start=k == 0, stop=k == (3 if a == 0 else 1))
                            filled(e, last)
                        elif kind == "xtr":
                            if a == 5:
                                if count := nth(("lnB", n, 0)):
                                    pe.wait_ge(ln_hat, count)
                                src = hbuf[:]
                            else:
                                if count := scaled(n, 2 if a == 3 and i == 1 else i):
                                    pe.wait_ge(ln_done, count)
                                src = xn[:, u]
                            bank = open_bank(e)
                            for dk in range(2):
                                for hf in range(2):
                                    k = 2 * dk + hf
                                    last = nc.tensor.transpose(bank[:, k * P:(k + 1) * P], src[:, hf, dk * P:(dk + 1) * P], ident[:])
                            filled(e, last)
                        elif kind == "ff1":
                            if i == 0:
                                wait_out(pe, ("xtr", n, 0))
                            bank = open_bank(e)
                            wu = w("u" + str(a), D if a == 3 else DF)
                            for c in range(2):
                                ch = 2 * i + c
                                for dk in range(2):
                                    last = nc.tensor.matmul(bank[:, c * S:(c + 1) * S], wu[:, dk, ch * P:(ch + 1) * P],
                                                            src_x[:, dk, :], start=dk == 0, stop=dk == 1)
                            filled(e, last)
                        elif kind == "ff2":
                            nch = 2 if a == 3 else 8
                            for j in range(nch // 2):
                                wait_out(pe, ("ff1", n, j))
                            bank = open_bank(e)
                            wd = w("d" + str(a), D)
                            for ch in range(nch):
                                last = nc.tensor.matmul(bank[:, 0:D], hT[:, ch, i * P:(i + 1) * P], wd[:, ch, :],
                                                        start=ch == 0, stop=ch == nch - 1)
                            filled(e, last)

                @block.scalar
                def _(act):
                    def read_bank(e):
                        wait_filled(act, e)
                        return ps_misc[:, win.bank[e][0], :]

                    def out_of_bank(e, last):
                        last.then_inc(misc_out[win.bank[e][0]], 1)

                    for e in win.order:
                        kind, n, i = e
                        a, u, rot = attention(n), n % NB, n % 2
                        if kind == "pqk" and a > 0:
                            bank = read_bank(e)
                            if count := nth(("mid", n - 1, i)):
                                act.wait_ge(lo_done, count)
                            if a == 1:
                                for a2 in range(2):
                                    last = nc.scalar.activation(xb[:, i, a2 * S:(a2 + 1) * S], bank[:, a2 * S:(a2 + 1) * S],
                                                                ACT.Identity, bias=col("qk"[i] + "1", a2))
                            else:
                                last = nc.scalar.activation(xb[:, i, :], bank, ACT.Copy)
                            out_of_bank(e, last)
                        elif kind == "pvv" and a > 1:
                            bank = read_bank(e)
                            out_of_bank(e, nc.scalar.activation(vaug[:, rot, :, :, 0:HD],
                                                                bank.rearrange("p (f s d) -> p f s d", f=2, s=H), ACT.Copy))
                        elif kind == "pvt":
                            bank = read_bank(e)
                            for hf in range(2):
                                dst = vaug[:, rot, i, 8 * hf:8 * hf + 8, :].rearrange("p (b h) w -> p h b w", h=2)
                                src = bank[:, hf * 256:(hf + 1) * 256].rearrange("p (h b w) -> p h b w", h=2, b=4)
                                last = nc.scalar.activation(dst, src, ACT.Copy)
                            out_of_bank(e, last)
                        elif kind == "ctr":
                            bank = read_bank(e)
                            if a == 3:
                                last = nc.scalar.activation(cT[:, rot].rearrange("p a b -> p (a b)"), bank, ACT.Copy)
                            else:
                                for dst, g, b in ((cT[:, rot], "gk", "bk"), (vT[:], "gv", "bv")):
                                    for dk in range(2):
                                        last = nc.scalar.activation(dst[:, dk, :], bank[:, dk * S:(dk + 1) * S], ACT.Identity,
                                                                    scale=col(g, dk), bias=col(b, dk))
                            out_of_bank(e, last)
                        elif kind == "st":
                            if count := nth(e):
                                act.wait_ge(st_done, count)
                            k = n * H + i
                            m, s = divmod(k - PT_SLOTS, H)
                            if count := nth(("pvg", m, s // 4)):
                                act.wait_ge(pv_done, count)
                            used = 3 * P if a == 2 else 2 * S
                            nc.scalar.activation(pt[:, k % PT_SLOTS].rearrange("p a b -> p (a b)")[:, 0:used],
                                                 ps_st[:, i % 2].rearrange("p a b -> p (a b)")[:, 0:used],
                                                 ACT.Exp, scale=SCALE).then_inc(exp_done, 1)
                        elif kind == "pvout":
                            if count := nth(("pvg", n, 2 * i + 1)):
                                act.wait_ge(pv_done, count)
                            wait_filled(act, ("otr", n - 1, 1))
                            nc.scalar.activation(ote[:, i], ps_pv[:, i], ACT.Copy).then_inc(ote_ready, 1)
                        elif kind == "ott" and a > 0:
                            out_of_bank(e, nc.scalar.activation(ot[:].rearrange("p a b -> p (a b)"), read_bank(e), ACT.Copy))
                        elif kind == "xtr":
                            bank = read_bank(e)
                            if a == 5:
                                for dk in range(2):
                                    last = nc.scalar.activation(xT[:, u % 2, dk, :], bank[:, dk * S:(dk + 1) * S], ACT.Identity,
                                                                scale=col("gh", dk), bias=col("bh", dk))
                            else:
                                last = nc.scalar.activation(xT[:, u % 2].rearrange("p a b -> p (a b)"), bank, ACT.Copy)
                            out_of_bank(e, last)
                        elif kind == "ff1":
                            bank = read_bank(e)
                            for c in range(2):
                                last = nc.scalar.activation(hT[:, 2 * i + c, :], bank[:, c * S:(c + 1) * S],
                                                            ACT.Tanh if a == 1 else ACT.Relu, bias=col("u" + str(a), 2 * i + c))
                            out_of_bank(e, last)

                @block.vector
                def _(dve):
                    chain = [0]

                    def link(ins):
                        chain[0] += 1
                        ins.then_inc(dve_link, 1)
                        dve.wait_ge(dve_link, chain[0])

                    def read_bank(e):
                        wait_filled(dve, e)
                        return ps_misc[:, win.bank[e][0], :]

                    def out_of_bank(e, last):
                        last.then_inc(misc_out[win.bank[e][0]], 1)

                    def moments(src, k, eps, done):
                        for hf in range(2):
                            last = nc.vector.bn_stats(stats[:, k, hf, :], src[:, hf, :])
                        link(last)
                        for hf in range(2):
                            last = nc.vector.bn_aggr(mv[:, k, hf, :], stats[:, k, hf, :])
                        link(last)
                        nc.vector.tensor_scalar(var[:, k, :], mv[:, k, :, 1], eps, None, ALU.add).then_inc(done, 1)

                    def normalise(dst, src, k, done):
                        for hf in range(2):
                            last = nc.vector.tensor_scalar(dst[:, hf, :], src[:, hf, :], mv[:, k, hf, 0:1], rstd[:, k, hf:hf + 1],
                                                           ALU.subtract, ALU.mult)
                        last.then_inc(done, 1)

                    for e in win.order:
                        kind, n, i = e
                        a, u, rot = attention(n), n % NB, n % 2
                        x = xn[:, u]
                        if kind == "pad":
                            if count := 16 * nth(e):
                                dve.wait_ge(pad_loaded, count)
                            nc.vector.tensor_scalar(pen_row[0:NB, :], pad_i[:], 0.0, NEG, ALU.is_equal,
                                                    ALU.mult).then_inc(pad_made, 1)
                        elif kind == "pqk" and a == 0:
                            bank = read_bank(e)
                            if count := nth(("mid", n - 1, i)):
                                dve.wait_ge(lo_done, count)
                            dst = xb[:, i, :].rearrange("p (h c r) -> p c h r", h=2, r=16)
                            out_of_bank(e, nc.vector.transpose(dst, bank.rearrange("p (c h r) -> p c h r", h=2, r=16)))
                        elif kind == "hi":
                            if a == 0:
                                if count := nth(("pqk", n, i), lambda m, j: attention(m) == 0):
                                    dve.wait_ge(xb_biased, count)
                            else:
                                wait_out(dve, ("pqk", n, i))
                            if count := written(n - 1, i):
                                dve.wait_ge(scr_written[(n - 1) % 2][i], count)
                            nc.vector.tensor_copy(parts[:, i, HI, :], xb[:, i, :]).then_inc(hi_done, 1)
                        elif kind == "mid":
                            if count := nth(("hi", n, i)):
                                dve.wait_ge(rest_done, count)
                            nc.vector.tensor_copy(parts[:, i, MID, :], xb[:, i, :]).then_inc(mid_done, 1)
                        elif kind == "e0":
                            wait_out(dve, ("pqk", n, 0))
                            for a2 in range(2):
                                last = nc.vector.tensor_scalar(q0blk[:, a2, :], headsel[:, a2, :], xb[:, 0, a2 * S:a2 * S + 1],
                                                               None, ALU.mult)
                            last.then_inc(q0_ready, 1)
                        elif kind == "len":
                            e0 = ("e0", n, 0)
                            bank = read_bank(e0)
                            if count := win.before(e, "ff2", lambda m, j: attention(m) == 3):
                                dve.wait_ge(ff3_done, count)
                            out_of_bank(e0, nc.vector.tensor_scalar(nonzero, bank[0:H, 0:S], 0.0, None, ALU.not_equal))
                            wait_out(dve, e0)
                            link(nc.vector.reduce_sum(length[:], nonzero, AX))
                            if count := stacked(n - 2, 1):
                                dve.wait_ge(stack_ready[rot][1], count)
                            nc.vector.tensor_scalar(pen16[:, rot, :], iota[:], length[:, 0:1], NEG, ALU.is_ge,
                                                    ALU.mult).then_inc(pen_ready, 1)
                        elif kind == "pvv" and a <= 1:
                            bank = read_bank(e)
                            if a == 1:
                                dve.wait_ge(tiles_loaded, 16 * pieces("tiles"))
                            bias = tile2("v" + str(a)).rearrange("p f (s d) -> p f s d", d=HD)
                            out_of_bank(e, nc.vector.tensor_tensor(vaug[:, rot, :, :, 0:HD],
                                                                   bank.rearrange("p (f s d) -> p f s d", f=2, s=H), bias, ALU.add))
                            if a == 0:
                                wait_out(dve, e)
                                for hf in range(2):
                                    last = nc.vector.transpose(vflip[:, hf, :].rearrange("p (h c r) -> p c h r", h=2, r=16),
                                                               vaug[:, rot, hf].rearrange("p s (h r) -> p s h r", r=16))
                                last.then_inc(v_flipped, 1)
                        elif kind == "ctr" and a == 3:
                            if count := 16 * nth(("load", n, 0), lambda m, j: attention(m) in (3, 5)):
                                dve.wait_ge(cn_loaded, count)
                            if count := nth(("msk", n - NB, 0)):
                                dve.wait_ge(msk_done, count)
                            for hf in range(2):
                                last = nc.vector.tensor_scalar(cn[:, hf, :], cn[:, hf, :], tmask[:, u, 1, hf:hf + 1], None, ALU.mult)
                            last.then_inc(cmask_done, 1)
                        elif kind == "clnA":
                            if count := 16 * nth(("load", n, 0), lambda m, j: attention(m) in (3, 5)):
                                dve.wait_ge(cn_loaded, count)
                            moments(cn, NB, EPS, cln_var)
                        elif kind == "clnB":
                            if count := nth(("clnA", n, 0)):
                                dve.wait_ge(cln_rstd, count)
                            normalise(cn, cn, NB, cln_hat)
                        elif kind == "nat":
                            if count := nth(e):
                                dve.wait_ge(nat_done, count)
                            if a in (0, 2):
                                for hf in range(2):
                                    keys = (hf + 1) * P if a == 2 else S
                                    scores = ps_nat[:, i % 2, hf, 0:keys]
                                    mask = causal[:, S - keys:S] if a == 2 else mask0[:, hf, :]
                                    last = nc.vector.tensor_tensor_reduce(scores, scores, mask, 1.0, FLOOR, ALU.add, ALU.max,
                                                                          accum_out=mraw[:, i // 8, hf, i % 8:i % 8 + 1])
                            else:
                                last = nc.vector.reduce_max(mraw[:, i // 8, :, i % 8], ps_nat[:, i % 2], AX)
                            last.then_inc(max_done, 1)
                        elif kind == "neg":
                            if count := nth(("nat", n, 8 * i + 7)):
                                dve.wait_ge(max_done, count)
                            nc.vector.tensor_scalar(negm[:, i, :].rearrange("p (s f) -> p s f", f=2),
                                                    mraw[:, i].rearrange("p f s -> p s f"), FLOOR, -1.0,
                                                    ALU.max, ALU.mult).then_inc(neg_done, 1)
                        elif kind == "nmt":
                            bank = read_bank(e)
                            if count := shifted(n - 1, i):
                                dve.wait_ge(shift_ready[(n - 1) % 2][i], count)
                            out_of_bank(e, nc.vector.tensor_copy(negm_t[:, i, :], bank[0:16, 0:P]))
                        elif kind == "otr":
                            bank = read_bank(e).rearrange("p (f s w) -> p f s w", f=2, w=32)
                            link(nc.vector.reciprocal(rec[:, i], bank[:, :, :, HD]))
                            if a in (2, 3):
                                if count := nth(("msk", n - NB, 0)):
                                    dve.wait_ge(msk_done, count)
                                m = tmask[:, u, a - 2, :].unsqueeze(2).to_broadcast([P, 2, H // 2])
                                link(nc.vector.tensor_tensor(rec[:, i], rec[:, i], m, ALU.mult))
                            if count := nth(("res", n - 1, 0)):
                                dve.wait_ge(res_done, count)
                            src = bank[:, :, :, 0:HD]
                            by = rec[:, i].unsqueeze(3).to_broadcast([P, 2, H // 2, HD])
                            if a == 0:
                                last = nc.vector.tensor_tensor(on0[:, :, 8 * i:8 * i + 8, 0:HD], src, by, ALU.mult)
                            elif a in (2, 3):
                                for hf in range(2):
                                    heads = on[:, hf, :].rearrange("p (a h d) -> p h a d", a=2, d=HD)
                                    last = nc.vector.tensor_tensor(heads[:, 4 * i:4 * i + 4], src[:, hf].rearrange("p (h a) d -> p h a d", a=2),
                                                                   by[:, hf].rearrange("p (h a) d -> p h a d", a=2), ALU.mult)
                            else:
                                dst = on[:].rearrange("p f (s d) -> p f s d", d=HD)
                                last = nc.vector.tensor_tensor(dst[:, :, 8 * i:8 * i + 8, :], src, by, ALU.mult)
                            out_of_bank(e, last)
                        elif kind == "ott" and a == 0:
                            wait_out(dve, ("otr", n, 0))
                            wait_out(dve, ("otr", n, 1))
                            wait_filled(dve, ("ff2", n // NU * NU - 1, 1))
                            for hf in range(2):
                                last = nc.vector.transpose(ot0[:, hf, :].rearrange("p (c s r) -> p s c r", c=2, r=16),
                                                           on0[:, hf].rearrange("p s (c r) -> p s c r", r=16))
                            last.then_inc(ot0_ready, 1)
                        elif kind == "opr":
                            bank = read_bank(e)
                            if a <= 1:
                                if count := nth(("pb", n, 0)):
                                    dve.wait_ge(bias_done, count)
                            else:
                                if count := scaled(n - NB, 2 if a == 4 else 0):
                                    dve.wait_ge(ln_done, count)
                            out_of_bank(e, nc.vector.tensor_tensor(x, bank.rearrange("p (f d) -> p f d", f=2), x, ALU.add))
                        elif kind == "lnA":
                            if a in (2, 3) and i == 0:
                                if count := nth(("res", n, 0)):
                                    dve.wait_ge(res_done, count)
                            elif a == 1 and i == 1:
                                wait_out(dve, ("ff2", n, 0))
                                wait_out(dve, ("ff2", n, 1))
                            elif a == 3 and i == 1:
                                if count := nth(("ff2", n, 1), lambda m, j: attention(m) == 3):
                                    dve.wait_ge(ff3_done, count)
                            elif a == 3 and i == 2:
                                if count := scaled(n, 1):
                                    dve.wait_ge(ln_done, count)
                            else:
                                wait_out(dve, ("opr", n, 0))
                            moments(x, u, 0.0 if a == 0 else EPS, ln_var)
                        elif kind == "lnB":
                            if count := nth(("lnA", n, i)):
                                dve.wait_ge(ln_rstd, count)
                            if a == 0:
                                link(nc.vector.tensor_scalar(rstd[:, u, :], rstd[:, u, :], 1e-8, None, ALU.add))
                                link(nc.vector.reciprocal(rstd[:, u, :], rstd[:, u, :]))
                            if a == 5:
                                wait_filled(dve, ("xtr", n - 1, 0) if u else ("ctr", n + NB - 1, 0))
                            normalise(hbuf if a == 5 else x, x, u, ln_hat)
                        elif kind == "ff2":
                            bank = read_bank(e)[:, 0:D]
                            if a == 3:
                                if count := win.before(e, "ff2", lambda m, j: attention(m) == 3):
                                    dve.wait_ge(ff3_done, count)
                                out_of_bank(e, nc.vector.tensor_tensor(zt[:], bank, tile("d3"), ALU.add))
                                wait_out(dve, e)
                                if count := scaled(n, 0):
                                    dve.wait_ge(ln_done, count)
                                nc.vector.scalar_tensor_tensor(x[:, i, :], zt[:], tmask[:, u, 0, i:i + 1], x[:, i, :],
                                                               op0=ALU.mult, op1=ALU.add).then_inc(ff3_done, 1)
                            else:
                                if count := nth(("pb", n, 1 if a == 1 else 0)):
                                    dve.wait_ge(bias_done, count)
                                out_of_bank(e, nc.vector.tensor_tensor(x[:, i, :], bank, x[:, i, :], ALU.add))
                        elif kind == "msk":
                            if count := scaled(n, 1 if a == 1 else 0):
                                dve.wait_ge(ln_done, count)
                            m = tmask[:, u, a - 1, :]
                            link(nc.vector.tensor_reduce(m, x, AX, ALU.max, apply_absolute_value=True))
                            nc.vector.tensor_scalar(m, m, 0.0, None, ALU.not_equal).then_inc(msk_done, 1)

                @block.gpsimd
                def _(pool):
                    chain = [0]

                    def link(ins):
                        chain[0] += 1
                        ins.then_inc(pool_link, 1)
                        pool.wait_ge(pool_link, chain[0])

                    for e in win.order:
                        kind, n, i = e
                        a, u, rot = attention(n), n % NB, n % 2
                        x = xn[:, u]
                        if a == 1 and kind == "pb":
                            pool.wait_ge(tiles_loaded, 16 * pieces("tiles"))
                        if kind == "pqk" and a == 0:
                            wait_out(pool, e)
                            v = xb[:, i, :].rearrange("p (h c r) -> p h c r", h=2, r=16)
                            bias = cols[:, COFF["qk0"]:COFF["qk0"] + 16].unsqueeze(1).unsqueeze(3).to_broadcast([P, 2, 16, 16])
                            nc.gpsimd.tensor_tensor(v, v, bias, ALU.add).then_inc(xb_biased, 1)
                        elif kind == "hi":
                            if count := nth(e):
                                pool.wait_ge(hi_done, count)
                            if a in (2, 3):
                                wait_filled(pool, ("e0", n, 0))
                            nc.gpsimd.tensor_tensor(xb[:, i, :], xb[:, i, :], parts[:, i, HI, :], ALU.subtract).then_inc(rest_done, 1)
                        elif kind == "mid":
                            if count := nth(e):
                                pool.wait_ge(mid_done, count)
                            nc.gpsimd.tensor_tensor(parts[:, i, LO, :], xb[:, i, :], parts[:, i, MID, :], ALU.subtract).then_inc(lo_done, 1)
                        elif kind == "pb":
                            if a == 0:
                                if count := 16 * nth(("ldx", n, 0), lambda m, j: m % NB == u):
                                    pool.wait_ge(x_loaded[u], count)
                                bias = tile2("o0")
                            elif a == 1 and i == 0:
                                wait_filled(pool, ("xtr", n - NB, 0))
                                bias = tile2("o1")
                            elif a == 1:
                                wait_filled(pool, ("xtr", n, 0))
                                bias = tile2("d1")
                            else:
                                if count := nth(("lnB", n, 0)):
                                    pool.wait_ge(ln_hat, count)
                                bias = tile2("d5")
                            nc.gpsimd.tensor_tensor(x, x, bias, ALU.add).then_inc(bias_done, 1)
                        elif kind == "res":
                            wait_out(pool, ("otr", n, 0))
                            wait_out(pool, ("otr", n, 1))
                            if count := scaled(n - NB, 1 if a == 2 else 0):
                                pool.wait_ge(ln_done, count)
                            nc.gpsimd.tensor_tensor(x, x, on[:], ALU.add).then_inc(res_done, 1)
                        elif kind == "lnA":
                            if count := nth(e):
                                pool.wait_ge(ln_var, count)
                            nc.gpsimd.tensor_tensor(rstd[:, u, :], var[:, u, :], half_pow[:, 1 if a == 0 else 0, :],
                                                    ALU.pow).then_inc(ln_rstd, 1)
                        elif kind == "clnA":
                            if count := nth(e):
                                pool.wait_ge(cln_var, count)
                            nc.gpsimd.tensor_tensor(rstd[:, NB, :], var[:, NB, :], half_pow[:, 0, :], ALU.pow).then_inc(cln_rstd, 1)
                        elif kind == "lnB" and a < 5:
                            if count := nth(e):
                                pool.wait_ge(ln_hat, count)
                            k = {0: "0", 4: "40"}.get(a, str(a) + str(i))
                            if a == 2:
                                k = "20"
                            link(nc.gpsimd.tensor_tensor(x, x, tile2("g" + k), ALU.mult))
                            nc.gpsimd.tensor_tensor(x, x, tile2("b" + k), ALU.add).then_inc(ln_done, 1)

            nc.all_engine_barrier(sems_to_clear=group_sems)

        run(HEAD, 0)
        with nc.Fori(0, ITERS - 1) as it:
            run(BODY, it)
        run(TAIL, ITERS - 1)



def _feat(wt, cols):
    k = wt.shape[0] // P
    return np.ascontiguousarray(wt[:, cols].reshape(k, P, -1).transpose(1, 0, 2)).reshape(P, -1)


def kernel(**inputs):
    import concourse.bacc as bacc
    from concourse.bass_utils import run_bass_kernel_spmd

    v = {k: np.asarray(a) for k, a in inputs.items()}
    plain = np.arange(D)
    by_a2_d_h8 = np.array([(a2 * 8 + h8) * HD + d for a2 in range(2) for d in range(HD) for h8 in range(8)])
    by_slot = np.array([(a2 * 8 + h8) * HD + d for h8 in range(8) for a2 in range(2) for d in range(HD)])
    positions = np.array([r * 16 + c for c in range(16) for r in range(16)])

    def vec(a, n):
        return a.reshape(n, P).T

    l1, l2, l3 = "L1_xattn_", "L2_xattn_", "L3_xattn_"
    wo0 = np.zeros((P, 4, D), np.float32)
    wo0_t = v["L0_xattn_Wo"].T
    for half in range(2):
        for c2 in range(2):
            for cp in range(4):
                c = half * 8 + cp * 2 + c2
                wo0[32 * cp:32 * cp + HD, half * 2 + c2] = wo0_t[c * HD:(c + 1) * HD]

    def heads(name):
        return v[l2 + name].transpose(1, 0, 2).reshape(D, D)

    inw, inb = v[l1 + "in_proj_w"], v[l1 + "in_proj_b"]
    w = {"q0": _feat(v["L0_xattn_Wq"].T, plain), "k0": _feat(v["L0_xattn_Wk"].T, plain),
         "v0": _feat(v["L0_xattn_Wv"].T, plain), "o0": wo0.reshape(P, -1),
         "q1": _feat(inw[:D].T, by_a2_d_h8), "k1": _feat(inw[D:2 * D].T, by_a2_d_h8), "v1": _feat(inw[2 * D:].T, by_slot),
         "o1": _feat(v[l1 + "out_proj_w"].T[by_slot], plain),
         "u1": _feat(v[l1 + "w1"].T, np.arange(DF)), "d1": _feat(v[l1 + "w2"].T, plain),
         "u3": _feat(v[l2 + "fc1_w"].T, plain), "d3": _feat(v[l2 + "fc2_w"].T, plain),
         "u5": _feat(v[l3 + "ffn_w1"].T, np.arange(DF)), "d5": _feat(v[l3 + "ffn_w2"].T, plain)}
    for a, k in ((2, "1"), (3, "2")):
        w[f"q{a}"], w[f"k{a}"] = _feat(heads("Wq" + k), by_a2_d_h8), _feat(heads("Wk" + k), by_a2_d_h8)
        w[f"v{a}"] = _feat(heads("Wv" + k), by_slot)
    for a, k in ((4, "sa_"), (5, "ca_")):
        w[f"q{a}"], w[f"k{a}"] = _feat(v[l3 + k + "wq"].T, by_a2_d_h8), _feat(v[l3 + k + "wk"].T, by_a2_d_h8)
        w[f"v{a}"] = _feat(v[l3 + k + "wv"].T, by_slot)
        w[f"o{a}"] = _feat(v[l3 + k + "wo"].T[by_slot], plain)
    tiles = {"v0": v["L0_xattn_bv"], "o0": v["L0_xattn_bo"], "g0": v["L0_xattn_gamma"], "b0": v["L0_xattn_beta"],
             "v1": inb[2 * D:][by_slot], "o1": v[l1 + "out_proj_b"], "g10": v[l1 + "ln1_w"], "b10": v[l1 + "ln1_b"],
             "d1": v[l1 + "b2"], "g11": v[l1 + "ln2_w"], "b11": v[l1 + "ln2_b"],
             "g20": v[l2 + "ln1_g"], "b20": v[l2 + "ln1_b"], "g30": v[l2 + "ln2_g"], "b30": v[l2 + "ln2_b"],
             "g31": v[l2 + "ln3_g"], "b31": v[l2 + "ln3_b"], "d3": v[l2 + "fc2_b"],
             "g32": v[l3 + "g_sa"], "b32": v[l3 + "b_sa"], "g40": v[l3 + "g_qca"], "b40": v[l3 + "b_qca"],
             "d5": v[l3 + "ffn_b2"]}
    bq, bk = v["L0_xattn_bq"].reshape(16, HD).T, v["L0_xattn_bk"].reshape(16, HD).T
    cols = {"qk0": np.tile(np.concatenate([bq, bk]), (4, 1)),
            "q1": vec(inb[:D][by_a2_d_h8], 2), "k1": vec(inb[D:2 * D][by_a2_d_h8], 2),
            "u1": vec(v[l1 + "b1"], 8), "u3": vec(v[l2 + "fc1_b"], 2), "u5": vec(v[l3 + "ffn_b1"], 8),
            "gk": vec(v[l3 + "g_kca"], 2), "bk": vec(v[l3 + "b_kca"], 2), "gv": vec(v[l3 + "g_vca"], 2),
            "bv": vec(v[l3 + "b_vca"], 2), "gh": vec(v[l3 + "g_out"], 2), "bh": vec(v[l3 + "b_out"], 2)}

    def tokens(a):
        return a.reshape(ITERS, NB, 2, P, D).transpose(0, 1, 3, 2, 4)

    def features(a):
        return a.reshape(ITERS, NB, S, 2, P).transpose(0, 1, 4, 3, 2)

    attn = v["mask_1x1xSxS2_ik0"][0, 0][positions][:, positions]
    halves = lambda m: m.reshape(2, P, S).transpose(1, 0, 2).reshape(P, 2 * S)
    later = (np.arange(P)[None, :] > np.arange(P)[:, None]).astype(np.float32)
    headsel = np.zeros((P, 2, H), np.float32)
    for p in range(P):
        for a2 in range(2):
            headsel[p, a2, (p % 8) * 2 + a2] = 1
    arrays = {
        "x": tokens(v["x"]), "x_t": features(v["x"]), "ctx": tokens(v["ctx_1024"]), "ctx_t": features(v["ctx_1024"]),
        "attn": np.stack([halves(attn), halves(attn.T)], 1),
        "causal": np.concatenate([np.zeros((P, S - P), np.float32), later, later.T], 1),
        "pad": v["mask_Bx1x1xS2_ik0"][:, 0, 0][:, positions].reshape(ITERS, NB, S),
        "weights": np.concatenate([w[k] for k, _ in WEIGHTS], 1),
        "tiles": np.stack([tiles[k] for k in TILES]),
        "cols": np.concatenate([cols[k] for k, _ in COLS], 1),
        "ident": np.eye(P, dtype=np.float32), "headsel": headsel,
        "iota": np.tile(np.arange(S, dtype=np.float32), (H, 1)),
        "half_pow": np.tile(np.array([[-0.5, -0.5], [0.5, 0.5]], np.float32), (P, 1, 1)),
    }
    arrays = {k: np.ascontiguousarray(a) for k, a in arrays.items()}
    nc = bacc.Bacc("TRN2", target_bir_lowering=False, num_devices=1, dynamic_dma_scratch_size=1024)
    t = {k: nc.dram_tensor("in_" + k, a.shape, mybir.dt.from_np(a.dtype), kind="ExternalInput").ap() for k, a in arrays.items()}
    t["out"] = nc.dram_tensor("out", (ITERS, NB, P, 2, D), F32, kind="ExternalOutput").ap()
    t["scratch"] = nc.dram_tensor("scratch", (2, 2, 3, HD, H, S), BF16, kind="Internal").ap()
    block_kernel(nc, t)
    r = run_bass_kernel_spmd(nc, [{"in_" + k: a for k, a in arrays.items()}], core_ids=[0])
    out = r.results[0]["out"]
    return np.ascontiguousarray(out.transpose(0, 1, 3, 2, 4)).reshape(B, S, D)
```
